# Optimizing a Trainium2 kernel written in Bass

```python
import numpy as np
import jax
import jax.numpy as jnp

def _softmax(x, axis=-1):
    return jax.nn.softmax(x, axis=axis)

def _gelu(x):
    return jax.nn.gelu(x, approximate=True)

def _silu(x):
    return jax.nn.silu(x)

def _sigmoid(x):
    return jax.nn.sigmoid(x)

def _layernorm(x, axis=-1, eps=1e-05):
    m = jnp.mean(x, axis=axis, keepdims=True)
    v = jnp.var(x, axis=axis, keepdims=True)
    return (x - m) / jnp.sqrt(v + eps)

def _scatter_add(tgt, idx, src, axis=0):
    return tgt.at[idx].add(src)

def _segment_sum(src, seg, n):
    return jax.ops.segment_sum(src, seg, n)
kernel_name = 'mk_gnn_preln_d2_gnn_r32_2222a7'

def setup_inputs(seed: int=0):
    np.random.seed(seed)
    _w = jnp.asarray

    def _rec_inputs():
        import jax
        import jax.numpy as jnp
        _gk = jax.random.key(seed)
        x = -0.0003713 + 1 * jax.random.normal(jax.random.fold_in(_gk, 1), (3125, 256), jnp.float32)
        _s = jax.random.randint(jax.random.fold_in(_gk, 2), (25000,), 0, 3125, jnp.int32)
        _d = jax.random.randint(jax.random.fold_in(_gk, 3), (25000,), 0, 3125, jnp.int32)
        _loop = jnp.arange(3125, dtype=jnp.int32)
        src = jnp.concatenate([_s, _d, _loop])
        dst = jnp.concatenate([_d, _s, _loop])
        _o = jnp.argsort(dst, stable=True)
        src = src[_o]
        dst = dst[_o]
        edge_type_8 = jax.random.randint(jax.random.fold_in(_gk, 13), (53125,), 0, 8, jnp.int32)
        edge_weight = jax.random.uniform(jax.random.fold_in(_gk, 14), (53125,), jnp.float32, 0.0, 0.999998)
        return (x, src, dst, edge_type_8, edge_weight)
    x, src, dst, edge_type_8, edge_weight = _rec_inputs()

    def _L0_gnn_setup():
        import jax, jax.numpy as jnp
        import numpy as np
        N = 50000
        F = 256
        E = 25000

        def _forward(X, edge_index, edge_weight, initial_weight, pool_p, gru_W_ih, gru_W_hh, gru_b_ih, gru_b_hh):
            n, f = X.shape
            score = X @ pool_p / jnp.linalg.norm(pool_p)
            top_vals, perm = jax.lax.top_k(score, f)
            X_tilde = X[perm] * jnp.tanh(top_vals)[:, None]
            h = initial_weight
            gi = X_tilde @ gru_W_ih.T + gru_b_ih
            gh = h @ gru_W_hh.T + gru_b_hh
            gi_r, gi_z, gi_n = jnp.split(gi, 3, axis=-1)
            gh_r, gh_z, gh_n = jnp.split(gh, 3, axis=-1)
            r = jax.nn.sigmoid(gi_r + gh_r)
            z = jax.nn.sigmoid(gi_z + gh_z)
            ncand = jnp.tanh(gi_n + r * gh_n)
            W = (1.0 - z) * ncand + z * h
            row, col = (edge_index[0], edge_index[1])
            loop = jnp.arange(n, dtype=edge_index.dtype)
            row = jnp.concatenate([row, loop])
            col = jnp.concatenate([col, loop])
            ew = jnp.concatenate([edge_weight, jnp.ones((n,), dtype=X.dtype)])
            deg = jax.ops.segment_sum(ew, col, num_segments=n)
            dinv = jnp.where(deg > 0, jax.lax.rsqrt(deg), 0.0)
            norm = dinv[row] * ew * dinv[col]
            xw = X @ W
            msgs = norm[:, None] * xw[row]
            out = jax.ops.segment_sum(msgs, col, num_segments=n)
            return out
        key = jax.random.key(seed)
        ks = jax.random.split(key, 10)
        X = jax.random.normal(ks[0], (N, F), dtype=jnp.float32)
        edge_index = jax.random.randint(ks[1], (2, E), 0, N, dtype=jnp.int64)
        edge_weight = jax.random.uniform(ks[2], (E,), dtype=jnp.float32)
        glorot = float(np.sqrt(6.0 / (F + F)))
        initial_weight = jax.random.uniform(ks[3], (F, F), minval=-glorot, maxval=glorot, dtype=jnp.float32)
        pool_p = jax.random.uniform(ks[4], (F,), minval=-glorot, maxval=glorot, dtype=jnp.float32)
        s = float(1.0 / np.sqrt(F))
        gru_W_ih = jax.random.uniform(ks[5], (3 * F, F), minval=-s, maxval=s, dtype=jnp.float32)
        gru_W_hh = jax.random.uniform(ks[6], (3 * F, F), minval=-s, maxval=s, dtype=jnp.float32)
        gru_b_ih = jax.random.uniform(ks[7], (3 * F,), minval=-s, maxval=s, dtype=jnp.float32)
        gru_b_hh = jax.random.uniform(ks[8], (3 * F,), minval=-s, maxval=s, dtype=jnp.float32)
        return {'X': X, 'edge_index': edge_index, 'edge_weight': edge_weight, 'initial_weight': initial_weight, 'pool_p': pool_p, 'gru_W_ih': gru_W_ih, 'gru_W_hh': gru_W_hh, 'gru_b_ih': gru_b_ih, 'gru_b_hh': gru_b_hh}
    _L0_gnn_all = _L0_gnn_setup()
    _L0_gnn_in = {k: v for k, v in _L0_gnn_all.items() if k in ('initial_weight', 'pool_p', 'gru_W_ih', 'gru_W_hh', 'gru_b_ih', 'gru_b_hh')}
    del _L0_gnn_all

    def _L1_gnn_setup():
        import jax, jax.numpy as jnp
        import numpy as np
        N_NODES = 625
        N_EDGES = 10000
        NUM_RELS = 8
        DIM = 256
        BN_EPS = 1e-05
        key = jax.random.key(seed)
        k1, k2, k3, k4, k5 = jax.random.split(key, 5)
        h = jax.random.normal(k1, (N_NODES, DIM), dtype=jnp.float32)
        weight = jax.random.normal(k2, (NUM_RELS, DIM, DIM), dtype=jnp.float32) * 0.05
        gamma = jnp.ones((DIM,), dtype=jnp.float32)
        beta = jnp.zeros((DIM,), dtype=jnp.float32)
        src = jax.random.randint(k3, (N_EDGES,), 0, N_NODES, dtype=jnp.int32)
        dst = jax.random.randint(k4, (N_EDGES,), 0, N_NODES, dtype=jnp.int32)
        rel = jax.random.randint(k5, (N_EDGES,), 0, NUM_RELS, dtype=jnp.int32)
        return {'h': h, 'weight': weight, 'gamma': gamma, 'beta': beta, 'src': src, 'dst': dst, 'rel': rel}
    _L1_gnn_all = _L1_gnn_setup()
    _L1_gnn_in = {k: v for k, v in _L1_gnn_all.items() if k in ('weight', 'gamma', 'beta')}
    del _L1_gnn_all
    return {'x': x, 'src': src, 'dst': dst, 'edge_type_8': edge_type_8, 'edge_weight': edge_weight, 'L0_gnn_initial_weight': _L0_gnn_in['initial_weight'], 'L0_gnn_pool_p': _L0_gnn_in['pool_p'], 'L0_gnn_gru_W_ih': _L0_gnn_in['gru_W_ih'], 'L0_gnn_gru_W_hh': _L0_gnn_in['gru_W_hh'], 'L0_gnn_gru_b_ih': _L0_gnn_in['gru_b_ih'], 'L0_gnn_gru_b_hh': _L0_gnn_in['gru_b_hh'], 'L1_gnn_weight': _L1_gnn_in['weight'], 'L1_gnn_gamma': _L1_gnn_in['gamma'], 'L1_gnn_beta': _L1_gnn_in['beta']}

def reference(x, src, dst, edge_type_8, edge_weight, L0_gnn_initial_weight, L0_gnn_pool_p, L0_gnn_gru_W_ih, L0_gnn_gru_W_hh, L0_gnn_gru_b_ih, L0_gnn_gru_b_hh, L1_gnn_weight, L1_gnn_gamma, L1_gnn_beta):
    import jax
    import jax.numpy as jnp

    def _L0_gnn_ref(X, edge_index, edge_weight, initial_weight, pool_p, gru_W_ih, gru_W_hh, gru_b_ih, gru_b_hh):
        import jax, jax.numpy as jnp
        import numpy as np
        N = 50000
        F = 256
        E = 25000

        def _forward(X, edge_index, edge_weight, initial_weight, pool_p, gru_W_ih, gru_W_hh, gru_b_ih, gru_b_hh):
            n, f = X.shape
            score = X @ pool_p / jnp.linalg.norm(pool_p)
            top_vals, perm = jax.lax.top_k(score, f)
            X_tilde = X[perm] * jnp.tanh(top_vals)[:, None]
            h = initial_weight
            gi = X_tilde @ gru_W_ih.T + gru_b_ih
            gh = h @ gru_W_hh.T + gru_b_hh
            gi_r, gi_z, gi_n = jnp.split(gi, 3, axis=-1)
            gh_r, gh_z, gh_n = jnp.split(gh, 3, axis=-1)
            r = jax.nn.sigmoid(gi_r + gh_r)
            z = jax.nn.sigmoid(gi_z + gh_z)
            ncand = jnp.tanh(gi_n + r * gh_n)
            W = (1.0 - z) * ncand + z * h
            row, col = (edge_index[0], edge_index[1])
            loop = jnp.arange(n, dtype=edge_index.dtype)
            row = jnp.concatenate([row, loop])
            col = jnp.concatenate([col, loop])
            ew = jnp.concatenate([edge_weight, jnp.ones((n,), dtype=X.dtype)])
            deg = jax.ops.segment_sum(ew, col, num_segments=n)
            dinv = jnp.where(deg > 0, jax.lax.rsqrt(deg), 0.0)
            norm = dinv[row] * ew * dinv[col]
            xw = X @ W
            msgs = norm[:, None] * xw[row]
            out = jax.ops.segment_sum(msgs, col, num_segments=n)
            return out
        return _forward(X, edge_index, edge_weight, initial_weight, pool_p, gru_W_ih, gru_W_hh, gru_b_ih, gru_b_hh)

    def _L1_gnn_ref(h, weight, gamma, beta, src, dst, rel):
        import jax, jax.numpy as jnp
        import numpy as np
        N_NODES = 625
        N_EDGES = 10000
        NUM_RELS = 8
        DIM = 256
        BN_EPS = 1e-05
        all_h = jnp.einsum('ni,rio->nro', h, weight)
        msg = all_h[src, rel]
        agg = jax.ops.segment_sum(msg, dst, num_segments=h.shape[0])
        mean = jnp.mean(agg, axis=0)
        var = jnp.mean(jnp.square(agg - mean), axis=0)
        out = (agg - mean) * jax.lax.rsqrt(var + BN_EPS) * gamma + beta
        return out
    edge_index = jnp.stack([src, dst])
    h = jnp.maximum(_layernorm(x, axis=-1), 0.0)
    x = x + _L0_gnn_ref(h, edge_index, edge_weight, L0_gnn_initial_weight, L0_gnn_pool_p, L0_gnn_gru_W_ih, L0_gnn_gru_W_hh, L0_gnn_gru_b_ih, L0_gnn_gru_b_hh)
    h = jnp.maximum(_layernorm(x, axis=-1), 0.0)
    x = x + _L1_gnn_ref(h, L1_gnn_weight, L1_gnn_gamma, L1_gnn_beta, src, dst, edge_type_8)
    return x

_drawn_inputs = setup_inputs


def setup_inputs(seed=0):
    import zlib

    import numpy as np

    out = dict(_drawn_inputs(seed))
    spreads = {'L1_gnn_gamma': (1.0, 0.6), 'L1_gnn_beta': (0.0, 0.587)}
    factors = {'L0_gnn_gru_W_hh': 6.545}
    for name, (base, spread) in spreads.items():
        noise = np.random.default_rng([zlib.crc32(name.encode()), seed]).standard_normal(out[name].shape)
        drawn = base * np.exp(spread * noise) if base else spread * noise
        out[name] = jnp.asarray(drawn.astype(out[name].dtype))
    for name, factor in factors.items():
        out[name] = (out[name] * factor).astype(out[name].dtype)
    return out
```

```python
import concourse.bass as bass
from concourse import mybir
from contextlib import ExitStack

N, F, E = 3125, 256, 53125
NREL = 8
P = 128
H = F // P
T = 125
NT = N // T
BPW = 4
EW = BPW * P
W = 64
NG = -(-E // EW)
WPI = 4
NIT = NG // WPI
NPASS = -(-N // W)
APAD = N + 75
SLOTS = WPI * BPW
CB = 26
NCH = BPW * NG // CB
EPS = 1e-5
MAGIC = 1.5 * 2 ** 23
FULL, LAST = NG - 1, E - (NG - 1) * EW
SPLIT = [(0, 112), (112, T)]
assert NT * T == N and NIT * WPI == NG and NCH * CB == BPW * NG and NG <= P


def gnn_kernel(nc, x, src, dst, rel, ew, w0, pool_p, wih, whh, bih, bhh, wrel, gamma, beta, out):
    f32, bf16, i32 = mybir.dt.float32, mybir.dt.bfloat16, mybir.dt.int32
    ALU, ACT, AX = mybir.AluOpType, mybir.ActivationFunctionType, mybir.AxisListType
    ds = bass.ds

    table1 = nc.dram_tensor("table1", (N, F), f32, kind="Internal").ap()
    table2 = nc.dram_tensor("table2", (N, NREL * F), f32, kind="Internal").ap()
    score_row = nc.dram_tensor("score_row", (NT, T), f32, kind="Internal").ap()
    table2_rows = table2.rearrange("n (r f) -> (n r) f", r=NREL)

    with ExitStack() as ctx:
        def sb(name, shape, dt):
            return ctx.enter_context(nc.sbuf_tensor(name, shape, dt))

        def sem(name):
            return ctx.enter_context(nc.semaphore(name))

        x_sb = sb("x_sb", [P, NT, F], f32)
        h_sb = sb("h_sb", [P, NT, F], f32)
        acc = sb("acc", [P, H, APAD], f32)
        ring = sb("ring", [P, SLOTS, F], f32)
        onehot = sb("onehot", [P, WPI, BPW, W], f32)
        idx_now = sb("idx_now", [P, WPI, BPW], i32)
        scr_a = sb("scr_a", [P, 8000], f32)
        scr_b = sb("scr_b", [P, 5120], f32)
        gru_t = sb("gru_t", [P, H, 14 * P], f32)
        rel_t = sb("rel_t", [P, BPW, NG], f32)
        ew_t = sb("ew_t", [P, BPW, NG], f32)
        src_t = sb("src_t", [P, BPW, NG + WPI], i32)
        idx2_t = sb("idx2_t", [P, BPW, NG + WPI], i32)
        lo_t = sb("lo_t", [P, BPW * NG], bf16)
        hi_t = sb("hi_t", [P, BPW * NG], bf16)
        ewp = sb("ewp", [P, 3, BPW * NG], bf16)
        ew_r = sb("ew_r", [P, 2, BPW * NG], f32)
        iota = sb("iota", [P, F], f32)
        iota_i = sb("iota_i", [P, F], i32)
        iota_w = sb("iota_w", [P, W], f32)
        ident = sb("ident", [P, P], f32)
        lower = sb("lower", [P, T], f32)
        ones = sb("ones", [1, P], f32)
        span = sb("span", [P, 4], f32)
        base_row = sb("base_row", [1, 2, NG], f32)
        base_i = sb("base_i", [1, NG], i32)
        flag = sb("flag", [1, 2], f32)
        passes = sb("passes", [1, 1], i32)
        mv = sb("mv", [P, NT, 2], f32)
        st6 = sb("st6", [P, NT, 6], f32)
        rstd = sb("rstd", [P, NT], f32)
        nbias = sb("nbias", [P, NT], f32)
        degs = sb("degs", [P, 3 * NT], f32)
        dinv = sb("dinv", [P, NT], f32)
        dtmp = sb("dtmp", [P, 4, NT], f32)
        pbc = sb("pbc", [P, F], f32)
        psq = sb("psq", [P, 4], f32)
        score = sb("score", [P, 2, NT], f32)
        score_t = sb("score_t", [NT, T], f32)
        cnt = sb("cnt", [P, NT, 4], f32)
        rank = sb("rank", [P, NT], f32)
        th = sb("th", [P, NT], f32)
        oh_rank = sb("oh_rank", [P, 4, F], f32)
        h0 = sb("h0", [P, H, F], f32)
        w_new = sb("w_new", [P, H, F], f32)
        brow = sb("brow", [1, 2, 3 * F], f32)
        h2 = sb("h2", [P, F], f32)
        h2_t = sb("h2_t", [P, H, T], f32)
        ln = sb("ln", [P, 12], f32)
        gb = sb("gb", [P, 2, H], f32)
        bn6 = sb("bn6", [P, H, 7, 6], f32)
        bn = sb("bn", [P, H, 8], f32)

        gru_raw = ring[:, :, :].rearrange("p s f -> p (s f)")[:, 0:12 * F].rearrange("p (a f) -> p a f", a=12)
        A16 = scr_a[:, :].bitcast(bf16)
        n_lo, n_hi = T * CB, NT * CB
        iota_rep = A16[:, 0:n_lo].rearrange("p (c b) -> p c b", b=CB)
        oh_lo = [A16[:, n_lo * (1 + i):n_lo * (2 + i)].rearrange("p (c b) -> p c b", b=CB) for i in range(2)]
        o = 3 * n_lo
        oh_hi = [A16[:, o + n_hi * i:o + n_hi * (i + 1)].rearrange("p (c b) -> p c b", b=CB) for i in range(2)]
        o += 2 * n_hi
        oh_ew = [A16[:, o + 3 * n_hi * i:o + 3 * n_hi * (i + 1)].rearrange("p (s c b) -> p s c b", s=3, b=CB)
                 for i in range(2)]
        hp = scr_a[:, 0:NT * F].rearrange("p (t f) -> p t f", t=NT)
        wr = scr_a[:, 0:H * NREL * F].rearrange("p (k n) -> p k n", k=H)

        def ebuf(i):
            return scr_b[0:NG, EW * i:EW * (i + 1)]
        dst_i, src_i, rel_i = (ebuf(i).bitcast(i32) for i in range(3))
        ew_g, dst_f, hi_g, lo_g, rel_g, src_g, idx2_g = (ebuf(i) for i in range(3, 10))
        s_all = scr_b[0:T, 0:N]
        junk = scr_b[:, N + 3:5120].bitcast(bf16)
        def gbuf(i, n):
            return scr_b[:, H * F * i:H * F * (i + n)].rearrange("p (m f) -> p m f", m=H)
        xt, rz, cand, gtmp = gbuf(0, 1), gbuf(1, 2), gbuf(3, 1), gbuf(4, 1)
        s_tile = scr_b[:, 2048:2048 + 5 * H * T].rearrange("p (j h n) -> p j h n", j=5, h=H)
        rows2 = scr_b[:, 0:4 * 512].rearrange("p (c n) -> p c n", c=4)

        bank = [ctx.enter_context(nc.psum_tensor(f"bank{i}", [P, 512], f32)) for i in range(8)]
        win = [bank[v][:, 0:H * W].rearrange("p (h w) -> p h w", h=H) for v in range(WPI)]

        edges_in, x_in, gru_in, pool_in, wrel_in, small_in = (sem(n) for n in (
            "edges_in", "x_in", "gru_in", "pool_in", "wrel_in", "small_in"))
        table1_out, scores_out, scores_in = sem("table1_out"), sem("scores_out"), sem("scores_in")
        table2_out = [sem("table2_out0"), sem("table2_out1")]
        result_out = sem("result_out")
        gathered = [[sem(f"gathered{L}_{v}") for v in range(WPI)] for L in range(2)]
        d_step, a_step, p_step = sem("dve_step"), sem("act_step"), sem("pool_step")
        gate_a, gate_p, gate_d = sem("gate_act"), sem("gate_pool"), sem("gate_dve")
        consts = sem("consts")
        edges_ready, pads_ready = sem("edges_ready"), sem("pads_ready")
        edges_turned, edges_kept_d, turned_kept = sem("edges_turned"), sem("edges_kept_d"), sem("turned_kept")
        gru_turned = sem("gru_turned")
        ln_var, ln_std, ln_ready, h_ready = (sem(n) for n in ("ln_var", "ln_std", "ln_ready", "h_ready"))
        lohi_ready, chunk_ready, chunk_summed = sem("lohi_ready"), sem("chunk_ready"), sem("chunk_summed")
        deg_ready, deg_root, dinv_ready = sem("deg_ready"), sem("deg_root"), sem("dinv_ready")
        hp_ready, hp_turned, acc_init = sem("hp_ready"), sem("hp_turned"), sem("acc_init")
        psq_ready, pnorm_ready = sem("psq_ready"), sem("pnorm_ready")
        score_ready, score_turned, score_kept, tanh_ready = (sem(n) for n in (
            "score_ready", "score_turned", "score_kept", "tanh_ready"))
        rank_hot, rank_used, xt_kept = (sem(n) for n in ("rank_hot", "rank_used", "xt_kept"))
        gates_ready, rz_ready, cand_in, cand_ready, w_ready = (sem(n) for n in (
            "gates_ready", "rz_ready", "cand_in", "cand_ready", "w_ready"))
        passes_ready = sem("passes_ready")
        idx_ready = [sem(f"idx_ready{L}") for L in range(2)]
        hot_ready = [sem(f"hot_ready{L}") for L in range(2)]
        win_summed = [sem(f"win_summed{L}") for L in range(2)]
        win_added = [sem(f"win_added{L}") for L in range(2)]
        pass_step = [sem(f"pass_step{L}") for L in range(2)]
        agg_done = [sem(f"agg_done{L}") for L in range(2)]
        tile_in, tile_mul, t_var, t_std, t_ln, h2_ready = (sem(n) for n in (
            "tile_in", "tile_mul", "t_var", "t_std", "t_ln", "h2_ready"))
        h2_turned, h2_kept, prod_ready, prod_kept_a, prod_kept_d = (sem(n) for n in (
            "h2_turned", "h2_kept", "prod_ready", "prod_kept_a", "prod_kept_d"))
        t_step, cleared = sem("tile_step"), sem("cleared")
        bn_var, bn_std, bn_ready = sem("bn_var"), sem("bn_std"), sem("bn_ready")
        fin_in, fin_turned, fin_ready = sem("fin_in"), sem("fin_turned"), sem("fin_ready")

        block = ctx.enter_context(nc.Block())

        EDGE_DMAS = 4 * 3 * 16

        @block.sync
        def _(sp):
            for a, b in ((dst, dst_i), (ew, ew_g), (src, src_i), (rel, rel_i)):
                sp.dma_start(b[0:FULL, :], a[0:FULL * EW].rearrange("(g e) -> g e", e=EW)).then_inc(edges_in, 16)
                sp.dma_start(b[FULL:NG, 0:LAST],
                             a[FULL * EW:E].rearrange("(g e) -> g e", g=1)).then_inc(edges_in, 16)
                sp.dma_start(b[FULL:NG, LAST:EW],
                             a[E - EW + LAST:E].rearrange("(g e) -> g e", g=1)).then_inc(edges_in, 16)
            for lo, hi in SPLIT:
                sp.dma_start(x_sb[lo:hi, :, :],
                             x.rearrange("(t p) f -> p t f", p=T)[lo:hi, :, :]).then_inc(x_in, 16)
            sp.dma_start(pbc[:, :], pool_p.rearrange("(a n) -> a n", a=1).broadcast_to([P, F])).then_inc(pool_in, 16)
            sp.dma_start(gru_raw[:, 0:6, :], wih.rearrange("(a p) f -> p a f", p=P)).then_inc(gru_in, 16)
            sp.dma_start(gru_raw[:, 6:12, :], whh.rearrange("(a p) f -> p a f", p=P)).then_inc(gru_in, 16)
            sp.dma_start(h0[:, :, :], w0.rearrange("(a p) f -> p a f", p=P)).then_inc(gru_in, 16)
            sp.dma_start(brow[:, 0, :], bih.rearrange("(a n) -> a n", a=1)).then_inc(small_in, 16)
            sp.dma_start(brow[:, 1, :], bhh.rearrange("(a n) -> a n", a=1)).then_inc(small_in, 16)
            for q, a in enumerate((gamma, beta)):
                for h in range(H):
                    sp.dma_start(gb[:, q, h:h + 1],
                                 a[P * h:P * (h + 1)].rearrange("(p a) -> p a", a=1)).then_inc(small_in, 16)
            sp.wait_ge(score_kept, 1)
            sp.dma_start(score_row[:, :], score_t[:, :]).then_inc(scores_out, 16)
            sp.wait_ge(scores_out, 16)
            for lo, hi in SPLIT:
                sp.dma_start(s_all[lo:hi, :], score_row.rearrange("(a t) p -> a (t p)", a=1)
                             .broadcast_to([hi - lo, N])).then_inc(scores_in, 16)
            for i in range(5):
                sp.wait_ge(hp_ready, 5 * (i + 1))
                for lo, hi in SPLIT:
                    sp.dma_start(table1.rearrange("(t p) f -> p t f", p=T)[lo:hi, 5 * i:5 * i + 5, :],
                                 hp[lo:hi, 5 * i:5 * i + 5, :]).then_inc(table1_out, 16)
            sp.wait_ge(table1_out, 16 * 10)
            sp.wait_ge(hp_turned, NT)
            for k in range(H):
                sp.dma_start(wr[:, k, :].rearrange("p (r o) -> p r o", r=NREL),
                             wrel[:, P * k:P * (k + 1), :].rearrange("r p o -> p r o")).then_inc(wrel_in, 16)
            with sp.Fori(0, NT) as t:
                for q in range(2):
                    sp.wait_ge(prod_kept_a, t * 2 + (q + 1))
                    sp.wait_ge(prod_kept_d, t * 2 + (q + 1))
                    for lo, hi in SPLIT:
                        sp.dma_start(table2[ds(t * T + lo, hi - lo), 1024 * q:1024 * (q + 1)],
                                     rows2[lo:hi, 2 * q:2 * q + 2, :].rearrange("p c n -> p (c n)")
                                     ).then_inc(table2_out[q], 16)
            with sp.Fori(0, NT // 5) as i:
                sp.wait_ge(fin_ready, i * 5 + 10)
                for lo, hi in SPLIT:
                    sp.dma_start(out[ds(i * (5 * T), 5 * T), :].rearrange("(t p) f -> p t f", p=T)[lo:hi, :, :],
                                 x_sb[lo:hi, ds(i * 5, 5), :]).then_inc(result_out, 16)
            sp.wait_ge(result_out, 16 * 2 * (NT // 5))

        @block.gpsimd
        def _(pool):
            n = [0]

            def step(ins):
                n[0] += 1
                ins.then_inc(p_step, 1)
                pool.wait_ge(p_step, n[0])

            step(pool.iota(iota_i[:, :], [[1, F]], base=0, channel_multiplier=0))
            pool.tensor_copy(iota[:, :], iota_i[:, :]).then_inc(consts, 1)
            step(pool.memset(ident[:, :], 0.0))
            pool.affine_select(out=ident[:, :], in_=ident[:, :], compare_op=ALU.not_equal, fill=1.0, base=0,
                               pattern=[[-1, P]], channel_multiplier=1).then_inc(consts, 1)
            pool.iota(iota_rep, [[1, T], [0, CB]], base=0, channel_multiplier=0,
                      allow_small_or_imprecise_dtypes=True).then_inc(consts, 1)
            step(pool.memset(lower[:, :], 1.0))
            pool.affine_select(out=lower[:, :], in_=lower[:, :], compare_op=ALU.is_gt, fill=0.0, base=0,
                               pattern=[[-1, T]], channel_multiplier=1).then_inc(consts, 1)
            pool.memset(ones[:, :], 1.0).then_inc(consts, 1)
            pool.memset(acc[:, :, N:APAD], 0.0).then_inc(consts, 1)
            pool.wait_ge(edges_ready, 1)
            pool.affine_select(out=rel_g, in_=rel_g, compare_op=ALU.is_ge, fill=-10000.0, base=E - 1,
                               pattern=[[-1, EW]], channel_multiplier=-EW).then_inc(pads_ready, 1)
            pool.affine_select(out=ew_g, in_=ew_g, compare_op=ALU.is_ge, fill=0.0, base=E - 1,
                               pattern=[[-1, EW]], channel_multiplier=-EW).then_inc(pads_ready, 1)

            def gather_rows(L, table):
                n_pass = pool.value_load(passes[0:1, 0:1], min_val=1, max_val=NPASS)
                with pool.Fori(0, n_pass) as w:
                    with pool.Fori(0, NIT) as i:
                        for v in range(WPI):
                            pool.wait_ge(idx_ready[L], (w * NIT + i) * WPI + (v + 1))
                            pool.sem_inc(gate_p, 1)
                            for k in range(BPW):
                                pool.indirect_dma_start(
                                    ring[:, BPW * v + k, :], None, table,
                                    bass.IndirectOffsetOnAxis(ap=idx_now[:, v, k:k + 1], axis=0),
                                ).then_inc(gathered[L][v], 16)

            pool.wait_ge(passes_ready, 1)
            pool.wait_ge(table1_out, 16 * 10)
            gather_rows(0, table1[:, :])
            pool.wait_ge(tile_in, NT)
            pool.memset(acc[:, :, :], 0.0).then_inc(cleared, 1)
            for q in range(2):
                pool.wait_ge(table2_out[q], 2 * 16 * NT)
            gather_rows(1, table2_rows)

        @block.scalar
        def _(act):
            for n, (b, to) in enumerate(((2, rel_t[:, :, :]), (3, ew_t[:, :, :]),
                                         (4, src_t[:, :, 0:NG]), (5, idx2_t[:, :, 0:NG]))):
                act.wait_ge(edges_turned, n + 3)
                act.activation(to, bank[b][:, 0:BPW * NG].rearrange("p (k g) -> p k g", k=BPW),
                               ACT.Copy).then_inc(turned_kept, 1)
            act.wait_ge(turned_kept, 4)
            for a in (src_t, idx2_t):
                act.activation(a[:, :, NG:NG + WPI], a[:, :, 0:WPI], ACT.Copy).then_inc(a_step, 1)
            for n in range(8):
                k, g = n // 4, n % 4
                c0, c1 = 512 * g, min(512 * (g + 1), 14 * P)
                act.wait_ge(gru_turned, n + 1)
                act.activation(gru_t[:, k, c0:c1], bank[2 + n % 4][:, 0:c1 - c0], ACT.Copy).then_inc(turned_kept, 1)
            act.wait_ge(ln_var, 1)
            act.activation(rstd[0:T, :], rstd[0:T, :], ACT.Sqrt).then_inc(ln_std, 1)
            act.wait_ge(psq_ready, 1)
            act.activation(psq[:, 1:2], psq[:, 0:1], ACT.Sqrt).then_inc(pnorm_ready, 1)
            act.wait_ge(ln_ready, 1)
            with act.Fori(0, NT // 5) as i:
                for j in range(5):
                    t = i * 5 + j
                    act.activation(h_sb[0:T, ds(t, 1), :].rearrange("p a f -> p (a f)"),
                                   x_sb[0:T, ds(t, 1), :].rearrange("p a f -> p (a f)"), ACT.Relu,
                                   bias=nbias[0:T, ds(t, 1)], scale=rstd[0:T, ds(t, 1)]).then_inc(h_ready, 1)
            act.wait_ge(deg_ready, 1)
            act.activation(dtmp[0:T, 2, :], dtmp[0:T, 1, :], ACT.Sqrt).then_inc(deg_root, 1)
            act.wait_ge(dinv_ready, 1)
            act.wait_ge(h_ready, NT)
            for t in range(NT):
                act.activation(hp[0:T, t, :], h_sb[0:T, t, :], ACT.Copy, scale=dinv[0:T, t:t + 1]).then_inc(hp_ready, 1)
            for t in range(NT):
                act.wait_ge(hp_turned, t + 1)
                act.activation(acc[:, :, T * t:T * (t + 1)],
                               bank[2 + t % 4][:, 0:H * T].rearrange("p (h n) -> p h n", h=H),
                               ACT.Copy).then_inc(acc_init, 1)
            act.wait_ge(score_ready, 1)
            act.activation(th[0:T, :], score[0:T, 1, :], ACT.Tanh).then_inc(tanh_ready, 1)
            for m in range(H):
                act.wait_ge(gates_ready, 2 * m + 1)
                act.activation(rz[:, m, :], bank[1 + m][:, :], ACT.Sigmoid).then_inc(rz_ready, 1)
            for m in range(H):
                act.wait_ge(cand_in, m + 1)
                act.activation(cand[:, m, :], gtmp[:, m, :], ACT.Tanh).then_inc(cand_ready, 1)

            def stage_indices(L, table):
                act.wait_ge(a_step, 2)
                for v in range(WPI):
                    act.activation(idx_now[:, v, :], table[:, :, v], ACT.Copy).then_inc(idx_ready[L], 1)
                n_pass = act.value_load(passes[0:1, 0:1], min_val=1, max_val=NPASS)
                with act.Fori(0, n_pass) as w:
                    with act.Fori(0, NIT) as i:
                        for v in range(WPI):
                            act.wait_ge(win_summed[L], (w * NIT + i) * WPI + (v + 1))
                            act.sem_inc(gate_a, 1)
                            act.activation(idx_now[:, v, :],
                                           table[:, :, ds(i * WPI + (WPI + v), 1)].rearrange("p k a -> p (k a)"),
                                           ACT.Copy).then_inc(idx_ready[L], 1)

            act.wait_ge(passes_ready, 1)
            stage_indices(0, src_t)
            act.wait_ge(agg_done[0], 1)

            def load_tile(t):
                act.activation(s_tile[:, 0, :, :], acc[:, :, ds(t * T, T)], ACT.Copy).then_inc(tile_in, 1)

            def root(n):
                act.wait_ge(t_var, n)
                act.sem_inc(gate_a, 1)
                act.activation(ln[0:T, 9:10], ln[0:T, 8:9], ACT.Sqrt).then_inc(t_std, 1)

            def norm(t, n):
                act.wait_ge(t_ln, n)
                act.sem_inc(gate_a, 1)
                act.activation(h2[0:T, :], x_sb[0:T, ds(t, 1), :].rearrange("p a f -> p (a f)"), ACT.Relu,
                               bias=ln[0:T, 11:12], scale=ln[0:T, 10:11]).then_inc(h2_ready, 1)

            def keep_products(t, first=False):
                act.wait_ge(h2_turned, t + 1)
                act.sem_inc(gate_a, 1)
                act.activation(h2_t[:, :, :], bank[5][:, 0:H * T].rearrange("p (h n) -> p h n", h=H),
                               ACT.Copy).then_inc(h2_kept, 1)
                for q in range(2):
                    act.wait_ge(prod_ready, t * 4 + (2 * q + 1))
                    if not first:
                        act.wait_ge(table2_out[q], t * 32)
                    act.sem_inc(gate_a, 1)
                    act.activation(rows2[0:T, 2 * q, :], bank[6][0:T, :], ACT.Copy).then_inc(prod_kept_a, 1)

            act.activation(s_tile[:, 0, :, :], acc[:, :, 0:T], ACT.Copy).then_inc(tile_in, 1)
            act.wait_ge(t_var, 1)
            act.activation(ln[0:T, 9:10], ln[0:T, 8:9], ACT.Sqrt).then_inc(t_std, 1)
            act.wait_ge(t_ln, 1)
            act.activation(h2[0:T, :], x_sb[0:T, 0, :], ACT.Relu, bias=ln[0:T, 11:12],
                           scale=ln[0:T, 10:11]).then_inc(h2_ready, 1)

            def tile_after(t, first=False):
                act.wait_ge(tile_mul, t + 1)
                act.sem_inc(gate_a, 1)
                load_tile(t + 1)
                keep_products(t, first)
                root(t + 2)
                norm(t + 1, t + 2)

            tile_after(0, True)
            with act.Fori(1, NT - 1) as t:
                tile_after(t)
            keep_products(NT - 1)

            stage_indices(1, idx2_t)
            act.wait_ge(bn_var, 1)
            act.activation(bn[:, :, 3], bn[:, :, 2], ACT.Sqrt).then_inc(bn_std, 1)
            act.wait_ge(bn_ready, 1)
            with act.Fori(0, NT // 5) as i:
                for j in range(5):
                    act.wait_ge(fin_turned, i * 5 + (j + 1))
                    act.sem_inc(gate_a, 1)
                    for h in range(H):
                        last = act.activation(s_tile[:, j, h, :], acc[:, h, ds(i * (5 * T) + j * T, T)], ACT.Identity,
                                              bias=bn[:, h, 6:7], scale=bn[:, h, 5:6])
                    last.then_inc(fin_in, 1)

        @block.vector
        def _(dve):
            n = [0]

            def step(ins):
                n[0] += 1
                ins.then_inc(d_step, 1)
                dve.wait_ge(d_step, n[0])

            dve.wait_ge(edges_in, EDGE_DMAS)
            step(dve.tensor_copy(dst_f, dst_i))
            dve.tensor_reduce(span[0:NG, 0:1], dst_f, AX.X, ALU.min)
            step(dve.tensor_reduce(span[0:NG, 1:2], dst_f, AX.X, ALU.max))
            dve.tensor_scalar(rel_g, dst_f, span[0:NG, 0:1], None, ALU.subtract).then_inc(edges_ready, 1)
            step(dve.tensor_tensor(span[0:NG, 2:3], span[0:NG, 1:2], span[0:NG, 0:1], ALU.subtract))
            step(dve.tensor_scalar(hi_g, dst_f, 1.0 / T, 0.5 / T - 0.5, ALU.mult, ALU.add))
            step(dve.tensor_scalar(hi_g, hi_g, MAGIC, MAGIC, ALU.add, ALU.subtract))
            step(dve.scalar_tensor_tensor(lo_g, hi_g, -float(T), dst_f, ALU.mult, ALU.add))
            step(dve.tensor_copy(src_g, src_i))
            dve.scalar_tensor_tensor(idx2_g, src_i, float(NREL), rel_i, ALU.mult, ALU.add).then_inc(edges_ready, 1)

            dve.wait_ge(x_in, 32)
            base = n[0]
            with dve.Fori(0, NT // 5) as i:
                for j in range(5):
                    t = i * 5 + j
                    dve.bn_stats(st6[0:T, ds(t, 1), :].rearrange("p a f -> p (a f)"),
                                 x_sb[0:T, ds(t, 1), :].rearrange("p a f -> p (a f)")).then_inc(d_step, 1)
            n[0] += NT
            dve.wait_ge(d_step, n[0])
            for t in range(NT):
                last = dve.bn_aggr(mv[0:T, t, :], st6[0:T, t, :])
            step(last)
            dve.tensor_scalar(rstd[0:T, :], mv[0:T, :, 1], EPS, None, ALU.add).then_inc(ln_var, 1)
            dve.wait_ge(pool_in, 16)
            dve.tensor_tensor_reduce(out=oh_rank[:, 0, :], in0=pbc[:, :], in1=pbc[:, :], scale=1.0, scalar=0.0,
                                     op0=ALU.mult, op1=ALU.add, accum_out=psq[:, 0:1]).then_inc(psq_ready, 1)
            dve.wait_ge(ln_std, 1)
            step(dve.reciprocal(rstd[0:T, :], rstd[0:T, :]))
            dve.scalar_tensor_tensor(nbias[0:T, :], mv[0:T, :, 0], -1.0, rstd[0:T, :], ALU.mult,
                                     ALU.mult).then_inc(ln_ready, 1)

            dve.wait_ge(edges_turned, 2)
            dve.tensor_copy(lo_t[:, :], bank[0][:, 0:BPW * NG])
            dve.tensor_copy(hi_t[:, :], bank[1][:, 0:BPW * NG]).then_inc(edges_kept_d, 1)
            dve.wait_ge(edges_turned, 7)
            dve.tensor_copy(base_row[:, 0, :], bank[6][0:1, 0:NG])
            step(dve.tensor_copy(base_row[:, 1, :], bank[6][0:1, 0:NG]))
            dve.tensor_copy(base_i[:, :], base_row[:, 0, :])
            step(dve.tensor_reduce(flag[:, 0:1], bank[6][0:1, P:P + NG], AX.X, ALU.max))
            step(dve.tensor_scalar(flag[:, 1:2], flag[:, 0:1], 1.0 / W, 0.5 / W - 0.5, ALU.mult, ALU.add))
            step(dve.tensor_scalar(flag[:, 1:2], flag[:, 1:2], MAGIC, MAGIC, ALU.add, ALU.subtract))
            dve.tensor_scalar(passes[:, :], flag[:, 1:2], 1.0, None, ALU.add).then_inc(passes_ready, 1)

            dve.wait_ge(turned_kept, 2)
            ewf = ew_t[:, :, :].rearrange("p k g -> p (k g)")
            step(dve.tensor_copy(ewp[:, 0, :], ewf))
            step(dve.tensor_tensor(ew_r[:, 0, :], ewf, ewp[:, 0, :], ALU.subtract))
            step(dve.tensor_copy(ewp[:, 1, :], ew_r[:, 0, :]))
            step(dve.tensor_tensor(ew_r[:, 1, :], ew_r[:, 0, :], ewp[:, 1, :], ALU.subtract))
            step(dve.tensor_copy(ewp[:, 2, :], ew_r[:, 1, :]))

            step(dve.memset(degs[0:T, :], 0.0))
            dve.wait_ge(consts, 6)
            dve.wait_ge(edges_kept_d, 1)
            base = n[0]
            with dve.Fori(0, NCH // 2) as i:
                for b in range(2):
                    c = i * (2 * CB) + b * CB
                    dve.tensor_tensor(oh_lo[b], iota_rep, lo_t[:, ds(c, CB)].unsqueeze(1).broadcast_to([P, T, CB]),
                                      ALU.is_equal)
                    dve.tensor_tensor(oh_hi[b], iota_rep[:, 0:NT, :],
                                      hi_t[:, ds(c, CB)].unsqueeze(1).broadcast_to([P, NT, CB]),
                                      ALU.is_equal).then_inc(d_step, 1)
                    dve.wait_ge(d_step, i * 8 + (base + 3 * b + 1))
                    for s in range(3):
                        last = dve.tensor_tensor(oh_ew[b][:, s, :, :], oh_hi[b],
                                                 ewp[:, s, ds(c, CB)].unsqueeze(1).broadcast_to([P, NT, CB]), ALU.mult)
                        if s < 2:
                            last.then_inc(d_step, 1)
                    last.then_inc(chunk_ready, 1)
                for b in range(2):
                    dve.wait_ge(chunk_summed, i * 2 + (b + 1))
                    dve.tensor_tensor(degs[0:T, :], degs[0:T, :], bank[b][0:T, 0:3 * NT], ALU.add).then_inc(d_step, 1)
                    dve.wait_ge(d_step, i * 8 + (base + 7 + b))
            n[0] += 4 * NCH
            step(dve.tensor_tensor(dtmp[0:T, 0, :], degs[0:T, NT:2 * NT], degs[0:T, 2 * NT:3 * NT], ALU.add))
            step(dve.tensor_tensor(dtmp[0:T, 0, :], dtmp[0:T, 0, :], degs[0:T, 0:NT], ALU.add))
            step(dve.tensor_scalar(dtmp[0:T, 0, :], dtmp[0:T, 0, :], 1.0, None, ALU.add))
            step(dve.tensor_scalar(dtmp[0:T, 3, :], dtmp[0:T, 0, :], 0.0, None, ALU.is_gt))
            dve.tensor_scalar(dtmp[0:T, 1, :], dtmp[0:T, 0, :], 1e-30, None, ALU.max).then_inc(deg_ready, 1)
            dve.wait_ge(deg_root, 1)
            step(dve.reciprocal(dinv[0:T, :], dtmp[0:T, 2, :]))
            dve.tensor_tensor(dinv[0:T, :], dinv[0:T, :], dtmp[0:T, 3, :], ALU.mult).then_inc(dinv_ready, 1)

            dve.wait_ge(h_ready, NT)
            base = n[0]
            for t in range(NT):
                if t >= 3:
                    dve.wait_ge(d_step, base + t - 2)
                last = dve.tensor_tensor_reduce(out=oh_rank[0:T, 1 + t % 3, :], in0=h_sb[0:T, t, :], in1=pbc[0:T, :],
                                                scale=1.0, scalar=0.0, op0=ALU.mult, op1=ALU.add,
                                                accum_out=score[0:T, 0, t:t + 1]).then_inc(d_step, 1)
            n[0] += NT
            dve.wait_ge(d_step, n[0])
            dve.wait_ge(pnorm_ready, 1)
            step(dve.reciprocal(psq[:, 2:3], psq[:, 1:2]))
            dve.tensor_scalar(score[0:T, 1, :], score[0:T, 0, :], psq[0:T, 2:3], None, ALU.mult).then_inc(score_ready, 1)
            dve.wait_ge(score_turned, 1)
            dve.tensor_copy(score_t[:, :], bank[6][0:NT, 0:T]).then_inc(score_kept, 1)
            step(dve.memset(cnt[0:T, :, :], 0.0))
            dve.wait_ge(scores_in, 32)
            for t in range(NT):
                s = score[0:T, 1, t:t + 1]
                if t < NT - 1:
                    step(dve.tensor_scalar(junk[0:T, 0:N - T * (t + 1)], s_all[:, T * (t + 1):N], s, 0.0,
                                           ALU.is_gt, ALU.add, accum_out=cnt[0:T, t, 0:1]))
                if t:
                    step(dve.tensor_scalar(junk[0:T, 0:T * t], s_all[:, 0:T * t], s, 0.0, ALU.is_ge, ALU.add,
                                           accum_out=cnt[0:T, t, 1:2]))
                step(dve.tensor_scalar(junk[0:T, 0:T], s_all[:, T * t:T * (t + 1)], s, 0.0, ALU.is_gt, ALU.add,
                                       accum_out=cnt[0:T, t, 2:3]))
                step(dve.scalar_tensor_tensor(junk[0:T, 0:T], s_all[:, T * t:T * (t + 1)], s, lower[0:T, :],
                                              ALU.is_equal, ALU.mult, accum_out=cnt[0:T, t, 3:4]))
            step(dve.tensor_reduce(rank[0:T, :], cnt[0:T, :, :], AX.X, ALU.add))
            dve.wait_ge(tanh_ready, 1)
            for t in range(NT):
                if t >= 4:
                    dve.wait_ge(rank_used, t - 3)
                dve.tensor_scalar(oh_rank[0:T, t % 4, :], iota[0:T, :], rank[0:T, t:t + 1], th[0:T, t:t + 1],
                                  ALU.is_equal, ALU.mult).then_inc(rank_hot, 1)
            dve.wait_ge(rank_used, NT)
            dve.tensor_copy(xt[:, 0, :], bank[0][:, 0:F]).then_inc(xt_kept, 1)
            dve.tensor_copy(xt[:, 1, :], bank[7][:, 0:F]).then_inc(xt_kept, 1)
            for m in range(H):
                dve.wait_ge(rz_ready, m + 1)
                dve.wait_ge(gates_ready, 2 * m + 2)
                step(dve.tensor_tensor(gtmp[:, m, :], rz[:, m, 0:F], bank[3 + m][:, F:2 * F], ALU.mult))
                dve.tensor_tensor(gtmp[:, m, :], gtmp[:, m, :], bank[3 + m][:, 0:F], ALU.add).then_inc(cand_in, 1)
            for m in range(H):
                dve.wait_ge(cand_ready, m + 1)
                step(dve.tensor_tensor(w_new[:, m, :], h0[:, m, :], cand[:, m, :], ALU.subtract))
                step(dve.tensor_tensor(w_new[:, m, :], w_new[:, m, :], rz[:, m, F:2 * F], ALU.mult))
                dve.tensor_tensor(w_new[:, m, :], w_new[:, m, :], cand[:, m, :], ALU.add).then_inc(w_ready, 1)

            def add_windows(L):
                step(dve.tensor_copy(iota_w[:, :], iota[:, 0:W]))
                if L:
                    step(dve.tensor_copy(base_i[:, :], base_row[:, 0, :]))
                    step(dve.tensor_copy(base_row[:, 1, :], base_row[:, 0, :]))
                n_pass = dve.value_load(passes[0:1, 0:1], min_val=1, max_val=NPASS)
                with dve.Fori(0, n_pass) as w:
                    with dve.Fori(0, NIT) as i:
                        base = [dve.value_load(base_i[0:1, ds(i * WPI + v, 1)], min_val=0, max_val=N)
                                for v in range(WPI)]
                        for v in range(WPI):
                            g = i * WPI + v
                            if L == 0:
                                for k in range(BPW):
                                    last = dve.tensor_scalar(onehot[:, v, k, :], iota_w[:, :], rel_t[:, k, ds(g, 1)],
                                                             ew_t[:, k, ds(g, 1)], ALU.is_equal, ALU.mult)
                            else:
                                last = dve.tensor_tensor(
                                    onehot[:, v, :, :], iota_w[:, :].unsqueeze(1).broadcast_to([P, BPW, W]),
                                    rel_t[:, :, ds(g, 1)].broadcast_to([P, BPW, W]), ALU.is_equal)
                            last.then_inc(hot_ready[L], 1)
                        for v in range(WPI):
                            at = acc[:, :, ds(base[v], W)]
                            dve.wait_ge(win_summed[L], (w * NIT + i) * WPI + (v + 1))
                            dve.tensor_tensor(at, at, win[v], ALU.add).then_inc(win_added[L], 1)
                            dve.wait_ge(win_added[L], (w * NIT + i) * WPI + (v + 1))
                    dve.tensor_scalar(iota_w[:, :], iota_w[:, :], float(W), None, ALU.add).then_inc(pass_step[L], 1)
                    dve.tensor_scalar(base_row[:, 1, :], base_row[:, 1, :], float(W), float(N), ALU.add,
                                      ALU.min).then_inc(pass_step[L], 1)
                    dve.wait_ge(pass_step[L], w * 3 + 2)
                    dve.sem_inc(gate_d, 1)
                    dve.tensor_copy(base_i[:, :], base_row[:, 1, :]).then_inc(pass_step[L], 1)
                    dve.wait_ge(pass_step[L], w * 3 + 3)
                    dve.sem_inc(gate_d, 1)

            dve.wait_ge(acc_init, NT)
            add_windows(0)
            dve.sem_inc(agg_done[0], 1)

            def tile_norm(t, row, m):
                xr = x_sb[0:T, t, :] if row is None else row
                dv = dinv[0:T, t:t + 1] if row is None else dinv[0:T, ds(t, 1)]
                dve.wait_ge(tile_mul, m)
                dve.scalar_tensor_tensor(xr, bank[4][0:T, 0:F], dv, xr, ALU.mult, ALU.add).then_inc(t_step, 1)
                dve.wait_ge(t_step, (m - 1) * 4 + 1)
                dve.sem_inc(gate_d, 1)
                dve.bn_stats(ln[0:T, 0:6], xr).then_inc(t_step, 1)
                dve.wait_ge(t_step, (m - 1) * 4 + 2)
                dve.sem_inc(gate_d, 1)
                dve.bn_aggr(ln[0:T, 6:8], ln[0:T, 0:6]).then_inc(t_step, 1)
                dve.wait_ge(t_step, (m - 1) * 4 + 3)
                dve.tensor_scalar(ln[0:T, 8:9], ln[0:T, 7:8], EPS, None, ALU.add).then_inc(t_var, 1)
                dve.wait_ge(t_std, m)
                dve.reciprocal(ln[0:T, 10:11], ln[0:T, 9:10]).then_inc(t_step, 1)
                dve.wait_ge(t_step, m * 4)
                dve.tensor_scalar(ln[0:T, 11:12], ln[0:T, 6:7], ln[0:T, 10:11], -1.0, ALU.mult, ALU.mult).then_inc(t_ln, 1)

            def keep_products(t, first=False):
                for q in range(2):
                    dve.wait_ge(prod_ready, t * 4 + (2 * q + 2))
                    if not first:
                        dve.wait_ge(table2_out[q], t * 32)
                    dve.sem_inc(gate_d, 1)
                    dve.tensor_copy(rows2[0:T, 2 * q + 1, :], bank[7][0:T, :]).then_inc(prod_kept_d, 1)

            tile_norm(0, None, 1)

            def tile_after(t, first=False):
                dve.wait_ge(h2_ready, t + 1)
                dve.sem_inc(gate_d, 1)
                tile_norm(t + 1, x_sb[0:T, ds(t + 1, 1), :].rearrange("p a f -> p (a f)"), t + 2)
                keep_products(t, first)

            tile_after(0, True)
            with dve.Fori(1, NT - 1) as t:
                tile_after(t)
            keep_products(NT - 1)

            dve.wait_ge(cleared, 1)
            add_windows(1)
            CH = [(c, min(c + 512, N)) for c in range(0, N, 512)]
            for h in range(H):
                for q, (lo, hi) in enumerate(CH):
                    last = dve.bn_stats(bn6[:, h, q, :], acc[:, h, lo:hi])
            step(last)
            for h in range(H):
                last = dve.bn_aggr(bn[:, h, 0:2], bn6[:, h, :, :].rearrange("p q s -> p (q s)"))
            step(last)
            dve.tensor_scalar(bn[:, :, 2], bn[:, :, 1], EPS, None, ALU.add).then_inc(bn_var, 1)
            dve.wait_ge(bn_std, 1)
            dve.wait_ge(small_in, 96)
            step(dve.reciprocal(bn[:, :, 4], bn[:, :, 3]))
            step(dve.tensor_tensor(bn[:, :, 5], bn[:, :, 4], gb[:, 0, :], ALU.mult))
            step(dve.tensor_tensor(bn[:, :, 7], bn[:, :, 0], bn[:, :, 5], ALU.mult))
            dve.tensor_tensor(bn[:, :, 6], gb[:, 1, :], bn[:, :, 7], ALU.subtract).then_inc(bn_ready, 1)
            dve.sem_inc(fin_ready, 5)
            with dve.Fori(0, NT // 5) as i:
                for j in range(5):
                    row = x_sb[0:T, ds(i * 5 + j, 1), :].rearrange("p a f -> p (a f)")
                    dve.wait_ge(fin_turned, i * 5 + (j + 6))
                    dve.tensor_tensor(row, row, bank[j][0:T, 0:F], ALU.add).then_inc(fin_ready, 1)

        @block.tensor
        def _(pe):
            pe.wait_ge(consts, 6)
            pe.wait_ge(edges_ready, 2)
            pe.wait_ge(pads_ready, 2)
            for b, a in enumerate((lo_g, hi_g, rel_g, ew_g, src_g, idx2_g)):
                for k in range(BPW):
                    last = pe.transpose(bank[b][:, NG * k:NG * (k + 1)], a[:, P * k:P * (k + 1)], ident[0:NG, 0:NG])
                last.then_inc(edges_turned, 1)
            pe.transpose(bank[6][0:1, 0:NG], span[0:NG, 0:1], ident[0:NG, 0:NG])
            pe.transpose(bank[6][0:1, P:P + NG], span[0:NG, 2:3], ident[0:NG, 0:NG]).then_inc(edges_turned, 1)
            pe.wait_ge(gru_in, 48)
            for n in range(8):
                k, g = n // 4, n % 4
                pe.wait_ge(turned_kept, n + 1)
                for q in range(4 * g, min(4 * g + 4, 14)):
                    a = gru_raw[:, q, P * k:P * (k + 1)] if q < 12 else h0[:, q - 12, P * k:P * (k + 1)]
                    last = pe.transpose(bank[2 + n % 4][:, P * (q - 4 * g):P * (q - 4 * g + 1)], a, ident[:, :])
                last.then_inc(gru_turned, 1)
            with pe.Fori(0, NCH // 2) as i:
                for b in range(2):
                    pe.wait_ge(chunk_ready, i * 2 + (b + 1))
                    for c in range(CB):
                        last = pe.matmul(bank[b][0:T, 0:3 * NT], oh_lo[b][:, :, c],
                                         oh_ew[b][:, :, :, c].rearrange("p s c -> p (s c)"),
                                         start=(c == 0), stop=(c == CB - 1))
                    last.then_inc(chunk_summed, 1)
            for t in range(NT):
                pe.wait_ge(hp_ready, t + 1)
                pe.wait_ge(turned_kept, 12)
                if t >= 4:
                    pe.wait_ge(acc_init, t - 3)
                for h in range(H):
                    last = pe.transpose(bank[2 + t % 4][:, T * h:T * (h + 1)], hp[0:T, t, P * h:P * (h + 1)],
                                        ident[0:T, 0:T])
                last.then_inc(hp_turned, 1)
            pe.wait_ge(score_ready, 1)
            pe.transpose(bank[6][0:NT, 0:T], score[0:T, 1, :], ident[0:T, 0:T]).then_inc(score_turned, 1)
            for t in range(NT):
                pe.wait_ge(rank_hot, t + 1)
                for h in range(H):
                    last = pe.matmul(bank[h * 7][:, 0:F], h_sb[0:T, t, P * h:P * (h + 1)], oh_rank[0:T, t % 4, :],
                                     start=(t == 0), stop=(t == NT - 1))
                last.then_inc(rank_used, 1)
            pe.wait_ge(xt_kept, 2)
            pe.wait_ge(small_in, 96)
            pe.wait_ge(acc_init, NT)
            for m in range(H):
                xs = [xt[:, k, P * m:P * (m + 1)] for k in range(H)]
                hs = [gru_t[:, k, 12 * P + P * m:12 * P + P * (m + 1)] for k in range(H)]
                for k in range(H):
                    pe.matmul(bank[1 + m][:, :], xs[k], gru_t[:, k, 0:2 * F], start=(k == 0), stop=False)
                    pe.matmul(bank[1 + m][:, :], hs[k], gru_t[:, k, 3 * F:5 * F], start=False, stop=False)
                pe.matmul(bank[1 + m][:, :], ones[:, :], brow[:, 0, 0:2 * F], start=False, stop=False)
                pe.matmul(bank[1 + m][:, :], ones[:, :], brow[:, 1, 0:2 * F], start=False, stop=True).then_inc(gates_ready, 1)
                for q, (a, c) in enumerate(((xs, 2 * F), (hs, 5 * F))):
                    o = bank[3 + m][:, F * q:F * (q + 1)]
                    for k in range(H):
                        pe.matmul(o, a[k], gru_t[:, k, c:c + F], start=(k == 0), stop=False)
                    last = pe.matmul(o, ones[:, :], brow[:, q, 2 * F:3 * F], start=False, stop=True)
                last.then_inc(gates_ready, 1)

            def sum_windows(L):
                n_pass = pe.value_load(passes[0:1, 0:1], min_val=1, max_val=NPASS)
                with pe.Fori(0, n_pass) as w:
                    with pe.Fori(0, NIT) as i:
                        for v in range(WPI):
                            pe.wait_ge(hot_ready[L], (w * NIT + i) * WPI + (v + 1))
                            pe.wait_ge(gathered[L][v], (w * NIT + i) * (16 * BPW) + 16 * BPW)
                            for h in range(H):
                                for k in range(BPW):
                                    last = pe.matmul(win[v][:, h, :], ring[:, BPW * v + k, P * h:P * (h + 1)],
                                                     onehot[:, v, k, :], start=(k == 0), stop=(k == BPW - 1))
                            last.then_inc(win_summed[L], 1)

            pe.wait_ge(passes_ready, 1)
            pe.wait_ge(w_ready, 2)
            sum_windows(0)

            def times_w(m):
                pe.wait_ge(tile_in, m)
                for h in range(H):
                    last = pe.matmul(bank[4][0:T, 0:F], s_tile[:, 0, h, :], w_new[:, h, :],
                                     start=(h == 0), stop=(h == H - 1))
                last.then_inc(tile_mul, 1)

            def turn_h2(m):
                pe.wait_ge(h2_ready, m)
                for h in range(H):
                    last = pe.transpose(bank[5][:, T * h:T * (h + 1)], h2[0:T, P * h:P * (h + 1)], ident[0:T, 0:T])
                last.then_inc(h2_turned, 1)

            def products(t, first):
                pe.wait_ge(h2_kept, t + 1)
                for q in range(4):
                    if q >= 2 or not first:
                        kept = prod_kept_a if q % 2 == 0 else prod_kept_d
                        pe.wait_ge(kept, t * 2 + q // 2)
                    for k in range(H):
                        last = pe.matmul(bank[6 + q % 2][0:T, :], h2_t[:, k, :], wr[:, k, 512 * q:512 * (q + 1)],
                                         start=(k == 0), stop=(k == H - 1))
                    last.then_inc(prod_ready, 1)

            pe.wait_ge(wrel_in, 32)
            times_w(1)
            turn_h2(1)
            times_w(2)
            products(0, True)
            with pe.Fori(1, NT - 1) as t:
                turn_h2(t + 1)
                times_w(t + 2)
                products(t, False)
            turn_h2(NT)
            products(NT - 1, False)

            sum_windows(1)
            pe.sem_inc(fin_turned, 5)
            with pe.Fori(0, NT // 5) as i:
                for j in range(5):
                    pe.wait_ge(fin_in, i * 5 + (j + 1))
                    pe.wait_ge(fin_ready, i * 5 + (j + 1))
                    for h in range(H):
                        last = pe.transpose(bank[j][0:T, P * h:P * (h + 1)], s_tile[:, j, h, :], ident[:, :])
                    last.then_inc(fin_turned, 1)


_INS = ['x', 'src', 'dst', 'edge_type_8', 'edge_weight', 'L0_gnn_initial_weight', 'L0_gnn_pool_p', 'L0_gnn_gru_W_ih',
        'L0_gnn_gru_W_hh', 'L0_gnn_gru_b_ih', 'L0_gnn_gru_b_hh', 'L1_gnn_weight', 'L1_gnn_gamma', 'L1_gnn_beta']
_OUTS = [((N, F), 'float32')]


def kernel(**inputs):
    import numpy as _np
    import concourse.bacc as _bacc
    from concourse import mybir as _mybir
    from concourse.bass_utils import run_bass_kernel_spmd as _run

    nc = _bacc.Bacc("TRN2", target_bir_lowering=False, num_devices=1)
    arrays, args = {}, []
    for name in _INS:
        a = _np.ascontiguousarray(inputs[name])
        arrays[f"in_{name}_dram"] = a
        args.append(nc.dram_tensor(f"in_{name}_dram", a.shape, _mybir.dt.from_np(a.dtype), kind="ExternalInput").ap())
    for i, (shape, dtype) in enumerate(_OUTS):
        dt = _mybir.dt.from_np(_np.dtype(dtype))
        args.append(nc.dram_tensor(f"out_{i}_dram", shape, dt, kind="ExternalOutput").ap())
    gnn_kernel(nc, *args)
    r = _run(nc, [arrays], core_ids=[0])
    return r.results[0]["out_0_dram"]
```

```python
import concourse.bass as bass
from concourse import mybir
from contextlib import ExitStack

N, F, E = 3125, 256, 53125
NREL = 8
P = 128
H = F // P
T = 125
NT = N // T
BPW = 4
EW = BPW * P
W = 40
NG = -(-E // EW)
WPI = 4
NIT = NG // WPI
NPASS = -(-N // W)
APAD = N + 75
SLOTS = WPI * BPW
CB = 26
NCH = BPW * NG // CB
EPS = 1e-5
RANKED = [[[0], [1], [2], [3]], [[4], [5], [6], [7]], [[8], [9], [10], [11, 12]],
          [[13, 14, 15], [16, 17, 18], [19, 20, 21], [22, 23, 24]]]
GRU_IT = len(RANKED)
FIRST_IT = GRU_IT + 1
MAGIC = 1.5 * 2 ** 23
FULL, LAST = NG - 1, E - (NG - 1) * EW
SPLIT = [(0, 112), (112, T)]
assert NT * T == N and NIT * WPI == NG and NCH * CB == BPW * NG and NG <= P


def gnn_kernel(nc, x, src, dst, rel, ew, w0, pool_p, wih, whh, bih, bhh, wrel, gamma, beta, out):
    f32, bf16, i32 = mybir.dt.float32, mybir.dt.bfloat16, mybir.dt.int32
    ALU, ACT, AX = mybir.AluOpType, mybir.ActivationFunctionType, mybir.AxisListType
    ds = bass.ds

    table1 = nc.dram_tensor("table1", (N, F), f32, kind="Internal").ap()
    table2 = nc.dram_tensor("table2", (N, NREL * F), f32, kind="Internal").ap()
    score_row = nc.dram_tensor("score_row", (NT, T), f32, kind="Internal").ap()
    table2_rows = table2.rearrange("n (r f) -> (n r) f", r=NREL)

    with ExitStack() as ctx:
        def sb(name, shape, dt):
            return ctx.enter_context(nc.sbuf_tensor(name, shape, dt))

        def sem(name):
            return ctx.enter_context(nc.semaphore(name))

        x_sb = sb("x_sb", [P, NT, F], f32)
        h_sb = sb("h_sb", [P, NT, F], f32)
        acc = sb("acc", [P, H, APAD], f32)
        ring = sb("ring", [P, SLOTS, F], f32)
        onehot = sb("onehot", [P, WPI, BPW, W], f32)
        idx_now = sb("idx_now", [P, WPI, BPW], i32)
        scr_a = sb("scr_a", [P, 8000], f32)
        scr_b = sb("scr_b", [P, 5120], f32)
        gru_t = sb("gru_t", [P, H, 14 * P], f32)
        rel_t = sb("rel_t", [P, BPW, NG], f32)
        ew_t = sb("ew_t", [P, BPW, NG], f32)
        src_t = sb("src_t", [P, BPW, NG + WPI], i32)
        idx2_t = sb("idx2_t", [P, BPW, NG + WPI], i32)
        lo_t = sb("lo_t", [P, BPW * NG], bf16)
        hi_t = sb("hi_t", [P, BPW * NG], bf16)
        ewp = sb("ewp", [P, 3, BPW * NG], bf16)
        ew_r = sb("ew_r", [P, 2, BPW * NG], f32)
        iota = sb("iota", [P, F], f32)
        iota_i = sb("iota_i", [P, F], i32)
        iota_w = sb("iota_w", [P, W], f32)
        ident = sb("ident", [P, P], f32)
        lower = sb("lower", [P, T], f32)
        ones = sb("ones", [1, P], f32)
        span = sb("span", [P, 4], f32)
        base_row = sb("base_row", [1, 2, NG], f32)
        base_i = sb("base_i", [1, NG], i32)
        flag = sb("flag", [1, 4], f32)
        passes = sb("passes", [1, 2], i32)
        least = sb("least", [1, 2, NIT + 16], f32)
        early = sb("early", [1, 3, NIT], f32)
        early_i = sb("early_i", [1, NIT], i32)
        zrow = sb("zrow", [1, P], f32)
        ones_b = sb("ones_b", [P, 1], bf16)
        cmp_out = sb("cmp_out", [P, 2, T], bf16)
        rtmp = sb("rtmp", [P, 2, NT], f32)
        outdone = sb("outdone", [P, NT], f32)
        mv = sb("mv", [P, NT, 2], f32)
        st6 = sb("st6", [P, NT, 6], f32)
        rstd = sb("rstd", [P, NT], f32)
        nbias = sb("nbias", [P, NT], f32)
        degs = sb("degs", [P, 3 * NT], f32)
        dinv = sb("dinv", [P, NT], f32)
        dtmp = sb("dtmp", [P, 4, NT], f32)
        pbc = sb("pbc", [P, F], f32)
        psq = sb("psq", [P, 4], f32)
        score = sb("score", [P, 2, NT], f32)
        score_t = sb("score_t", [NT, T], f32)
        cnt = sb("cnt", [P, NT, 4], f32)
        rank = sb("rank", [P, NT], f32)
        th = sb("th", [P, NT], f32)
        oh_rank = sb("oh_rank", [P, 4, F], f32)
        h0 = sb("h0", [P, H, F], f32)
        w_new = sb("w_new", [P, H, F], f32)
        brow = sb("brow", [1, 2, 3 * F], f32)
        h2 = sb("h2", [P, F], f32)
        h2_t = sb("h2_t", [P, H, T], f32)
        ln = sb("ln", [P, 12], f32)
        gb = sb("gb", [P, 2, H], f32)
        bn6 = sb("bn6", [P, H, 7, 6], f32)
        bn = sb("bn", [P, H, 8], f32)

        gru_raw = ring[:, :, :].rearrange("p s f -> p (s f)")[:, 0:12 * F].rearrange("p (a f) -> p a f", a=12)
        A16 = scr_a[:, :].bitcast(bf16)
        n_lo, n_hi = T * CB, NT * CB
        iota_rep = A16[:, 0:n_lo].rearrange("p (c b) -> p c b", b=CB)
        oh_lo = [A16[:, n_lo * (1 + i):n_lo * (2 + i)].rearrange("p (c b) -> p c b", b=CB) for i in range(2)]
        o = 3 * n_lo
        oh_hi = [A16[:, o + n_hi * i:o + n_hi * (i + 1)].rearrange("p (c b) -> p c b", b=CB) for i in range(2)]
        o += 2 * n_hi
        oh_ew = [A16[:, o + 3 * n_hi * i:o + 3 * n_hi * (i + 1)].rearrange("p (s c b) -> p s c b", s=3, b=CB)
                 for i in range(2)]
        hp = scr_a[:, 0:NT * F].rearrange("p (t f) -> p t f", t=NT)
        wr = scr_a[:, 0:H * NREL * F].rearrange("p (k n) -> p k n", k=H)

        def ebuf(i):
            return scr_b[0:NG, EW * i:EW * (i + 1)]
        dst_i, src_i, rel_i = (ebuf(i).bitcast(i32) for i in range(3))
        ew_g, dst_f, hi_g, lo_g, rel_g, src_g, idx2_g = (ebuf(i) for i in range(3, 10))
        s_all = scr_b[0:T, 0:N]
        mask = [scr_b[:, N + 3:5120].bitcast(bf16), scr_a[:, NT * F:8000].bitcast(bf16)]
        def gbuf(i, n):
            return scr_b[:, H * F * i:H * F * (i + n)].rearrange("p (m f) -> p m f", m=H)
        xt, rz, cand, gtmp = gbuf(0, 1), gbuf(1, 2), gbuf(3, 1), gbuf(4, 1)
        s_tile = scr_b[:, 2048:2048 + 5 * H * T].rearrange("p (j h n) -> p j h n", j=5, h=H)
        rows2 = scr_b[:, 0:4 * 512].rearrange("p (c n) -> p c n", c=4)

        bank = [ctx.enter_context(nc.psum_tensor(f"bank{i}", [P, 512], f32)) for i in range(8)]
        win = [bank[v][:, 0:H * W].rearrange("p (h w) -> p h w", h=H) for v in range(WPI)]

        beaten = [bank[5 - b][0:T, 0:NT] for b in range(2)]

        edges_in, x_in, gru_in, pool_in, wrel_in, small_in = (sem(n) for n in (
            "edges_in", "x_in", "gru_in", "pool_in", "wrel_in", "small_in"))
        table1_out, scores_out, scores_in = sem("table1_out"), sem("scores_out"), sem("scores_in")
        table2_out = [sem("table2_out0"), sem("table2_out1")]
        result_out = sem("result_out")
        gathered = [[sem(f"gathered{L}_{v}") for v in range(WPI)] for L in range(2)]
        d_step, a_step, p_step = sem("dve_step"), sem("act_step"), sem("pool_step")
        gate_a, gate_p, gate_d, gate_pe = sem("gate_act"), sem("gate_pool"), sem("gate_dve"), sem("gate_pe")
        consts = sem("consts")
        edges_ready, pads_ready = sem("edges_ready"), sem("pads_ready")
        edges_turned, edges_kept_d, turned_kept = sem("edges_turned"), sem("edges_kept_d"), sem("turned_kept")
        gru_turned = sem("gru_turned")
        ln_var, ln_std, ln_ready, h_ready = (sem(n) for n in ("ln_var", "ln_std", "ln_ready", "h_ready"))
        lohi_ready, chunk_ready, chunk_summed = sem("lohi_ready"), sem("chunk_ready"), sem("chunk_summed")
        deg_ready, deg_root, dinv_ready = sem("deg_ready"), sem("deg_root"), sem("dinv_ready")
        hp_ready, hp_turned, acc_init = sem("hp_ready"), sem("hp_turned"), sem("acc_init")
        psq_ready, pnorm_ready = sem("psq_ready"), sem("pnorm_ready")
        score_ready, score_turned, score_kept, tanh_ready = (sem(n) for n in (
            "score_ready", "score_turned", "score_kept", "tanh_ready"))
        rank_hot, rank_used, xt_kept = (sem(n) for n in ("rank_hot", "rank_used", "xt_kept"))
        gates_ready, rz_ready, cand_in, cand_ready, w_ready = (sem(n) for n in (
            "gates_ready", "rz_ready", "cand_in", "cand_ready", "w_ready"))
        passes_ready = sem("passes_ready")
        idx_ready = [sem(f"idx_ready{L}") for L in range(2)]
        hot_ready = [sem(f"hot_ready{L}") for L in range(2)]
        win_summed = [sem(f"win_summed{L}") for L in range(2)]
        win_added = [sem(f"win_added{L}") for L in range(2)]
        pass_step = [sem(f"pass_step{L}") for L in range(2)]
        agg_done = [sem(f"agg_done{L}") for L in range(2)]
        tile_in, tile_mul, t_var, t_std, t_ln, h2_ready = (sem(n) for n in (
            "tile_in", "tile_mul", "t_var", "t_std", "t_ln", "h2_ready"))
        rows_free = [sem("rows_free0"), sem("rows_free1")]
        mask_ready, mask_used, counts_added, deg_summed = (sem(n) for n in (
            "mask_ready", "mask_used", "counts_added", "deg_summed"))
        h2_turned, h2_kept, prod_ready, prod_kept_a, prod_kept_d = (sem(n) for n in (
            "h2_turned", "h2_kept", "prod_ready", "prod_kept_a", "prod_kept_d"))
        t_step, cleared = sem("tile_step"), sem("cleared")
        bn_var, bn_std, bn_ready = sem("bn_var"), sem("bn_std"), sem("bn_ready")
        fin_in, fin_turned, fin_ready = sem("fin_in"), sem("fin_turned"), sem("fin_ready")

        block = ctx.enter_context(nc.Block())

        EDGE_DMAS = 4 * 3 * 16

        @block.sync
        def _(sp):
            for a, b in ((dst, dst_i), (ew, ew_g), (src, src_i), (rel, rel_i)):
                sp.dma_start(b[0:FULL, :], a[0:FULL * EW].rearrange("(g e) -> g e", e=EW)).then_inc(edges_in, 16)
                sp.dma_start(b[FULL:NG, 0:LAST],
                             a[FULL * EW:E].rearrange("(g e) -> g e", g=1)).then_inc(edges_in, 16)
                sp.dma_start(b[FULL:NG, LAST:EW],
                             a[E - EW + LAST:E].rearrange("(g e) -> g e", g=1)).then_inc(edges_in, 16)
            for lo, hi in SPLIT:
                sp.dma_start(x_sb[lo:hi, :, :],
                             x.rearrange("(t p) f -> p t f", p=T)[lo:hi, :, :]).then_inc(x_in, 16)
            sp.dma_start(pbc[:, :], pool_p.rearrange("(a n) -> a n", a=1).broadcast_to([P, F])).then_inc(pool_in, 16)
            sp.dma_start(gru_raw[:, 0:6, :], wih.rearrange("(a p) f -> p a f", p=P)).then_inc(gru_in, 16)
            sp.dma_start(gru_raw[:, 6:12, :], whh.rearrange("(a p) f -> p a f", p=P)).then_inc(gru_in, 16)
            sp.dma_start(h0[:, :, :], w0.rearrange("(a p) f -> p a f", p=P)).then_inc(gru_in, 16)
            sp.dma_start(brow[:, 0, :], bih.rearrange("(a n) -> a n", a=1)).then_inc(small_in, 16)
            sp.dma_start(brow[:, 1, :], bhh.rearrange("(a n) -> a n", a=1)).then_inc(small_in, 16)
            for q, a in enumerate((gamma, beta)):
                for h in range(H):
                    sp.dma_start(gb[:, q, h:h + 1],
                                 a[P * h:P * (h + 1)].rearrange("(p a) -> p a", a=1)).then_inc(small_in, 16)
            sp.wait_ge(score_kept, 1)
            sp.dma_start(score_row[:, :], score_t[:, :]).then_inc(scores_out, 16)
            sp.wait_ge(scores_out, 16)
            for lo, hi in SPLIT:
                sp.dma_start(s_all[lo:hi, :], score_row.rearrange("(a t) p -> a (t p)", a=1)
                             .broadcast_to([hi - lo, N])).then_inc(scores_in, 16)
            for i in range(5):
                sp.wait_ge(hp_ready, 5 * (i + 1))
                for lo, hi in SPLIT:
                    sp.dma_start(table1.rearrange("(t p) f -> p t f", p=T)[lo:hi, 5 * i:5 * i + 5, :],
                                 hp[lo:hi, 5 * i:5 * i + 5, :]).then_inc(table1_out, 16)
            sp.wait_ge(table1_out, 16 * 10)
            sp.wait_ge(hp_turned, NT)
            for k in range(H):
                sp.dma_start(wr[:, k, :].rearrange("p (r o) -> p r o", r=NREL),
                             wrel[:, P * k:P * (k + 1), :].rearrange("r p o -> p r o")).then_inc(wrel_in, 16)
            for q in range(2):
                sp.sem_inc(rows_free[q], 1)
            with sp.Fori(0, NT) as t:
                for q in range(2):
                    sp.wait_ge(prod_kept_a, t * 2 + (q + 2))
                    sp.wait_ge(prod_kept_d, t * 2 + (q + 2))
                    for lo, hi in SPLIT:
                        sp.dma_start(table2[ds(t * T + lo, hi - lo), 1024 * q:1024 * (q + 1)],
                                     rows2[lo:hi, 2 * q:2 * q + 2, :].rearrange("p c n -> p (c n)")
                                     ).then_inc(table2_out[q], 16)
                for q in range(2):
                    sp.wait_ge(table2_out[q], t * 32 + 32)
                    sp.sem_inc(rows_free[q], 1)
            with sp.Fori(0, NT // 5) as i:
                sp.wait_ge(fin_ready, i * 5 + 10)
                for lo, hi in SPLIT:
                    sp.dma_start(out[ds(i * (5 * T), 5 * T), :].rearrange("(t p) f -> p t f", p=T)[lo:hi, :, :],
                                 x_sb[lo:hi, ds(i * 5, 5), :]).then_inc(result_out, 16)
            sp.wait_ge(result_out, 16 * 2 * (NT // 5))

        @block.gpsimd
        def _(pool):
            n = [0]

            def step(ins):
                n[0] += 1
                ins.then_inc(p_step, 1)
                pool.wait_ge(p_step, n[0])

            step(pool.iota(iota_i[:, :], [[1, F]], base=0, channel_multiplier=0))
            pool.tensor_copy(iota[:, :], iota_i[:, :]).then_inc(consts, 1)
            step(pool.memset(ident[:, :], 0.0))
            pool.affine_select(out=ident[:, :], in_=ident[:, :], compare_op=ALU.not_equal, fill=1.0, base=0,
                               pattern=[[-1, P]], channel_multiplier=1).then_inc(consts, 1)
            pool.iota(iota_rep, [[1, T], [0, CB]], base=0, channel_multiplier=0,
                      allow_small_or_imprecise_dtypes=True).then_inc(consts, 1)
            step(pool.memset(lower[:, :], 1.0))
            pool.affine_select(out=lower[:, :], in_=lower[:, :], compare_op=ALU.is_gt, fill=0.0, base=0,
                               pattern=[[-1, T]], channel_multiplier=1).then_inc(consts, 1)
            pool.memset(ones[:, :], 1.0).then_inc(consts, 1)
            pool.memset(zrow[:, :], 0.0).then_inc(consts, 1)
            pool.memset(ones_b[:, :], 1.0).then_inc(consts, 1)
            pool.memset(acc[:, :, N:APAD], 0.0).then_inc(consts, 1)
            pool.wait_ge(edges_ready, 1)
            pool.affine_select(out=rel_g, in_=rel_g, compare_op=ALU.is_ge, fill=-10000.0, base=E - 1,
                               pattern=[[-1, EW]], channel_multiplier=-EW).then_inc(pads_ready, 1)
            pool.affine_select(out=ew_g, in_=ew_g, compare_op=ALU.is_ge, fill=0.0, base=E - 1,
                               pattern=[[-1, EW]], channel_multiplier=-EW).then_inc(pads_ready, 1)

            def gather_rows(L, table):
                n_pass = pool.value_load(passes[0:1, 0:1], min_val=1, max_val=NPASS)
                with pool.Fori(0, n_pass) as w:
                    with pool.Fori(0, NIT) as i:
                        for v in range(WPI):
                            pool.wait_ge(idx_ready[L], (w * NIT + i) * WPI + (v + 1))
                            pool.sem_inc(gate_p, 1)
                            for k in range(BPW):
                                pool.indirect_dma_start(
                                    ring[:, BPW * v + k, :], None, table,
                                    bass.IndirectOffsetOnAxis(ap=idx_now[:, v, k:k + 1], axis=0),
                                ).then_inc(gathered[L][v], 16)

            pool.wait_ge(passes_ready, 1)
            pool.wait_ge(table1_out, 16 * 10)
            gather_rows(0, table1[:, :])
            pool.wait_ge(tile_in, NT)
            pool.memset(acc[:, :, :], 0.0).then_inc(cleared, 1)
            for q in range(2):
                pool.wait_ge(table2_out[q], 2 * 16 * NT)
            gather_rows(1, table2_rows)

        @block.scalar
        def _(act):
            for n, (b, to) in enumerate(((2, rel_t[:, :, :]), (3, ew_t[:, :, :]),
                                         (4, src_t[:, :, 0:NG]), (5, idx2_t[:, :, 0:NG]))):
                act.wait_ge(edges_turned, n + 3)
                act.activation(to, bank[b][:, 0:BPW * NG].rearrange("p (k g) -> p k g", k=BPW),
                               ACT.Copy).then_inc(turned_kept, 1)
            act.wait_ge(turned_kept, 4)
            for a in (src_t, idx2_t):
                act.activation(a[:, :, NG:NG + WPI], a[:, :, 0:WPI], ACT.Copy).then_inc(a_step, 1)
            for n in range(8):
                k, g = n // 4, n % 4
                c0, c1 = 512 * g, min(512 * (g + 1), 14 * P)
                act.wait_ge(gru_turned, n + 1)
                act.activation(gru_t[:, k, c0:c1], bank[2 + n % 4][:, 0:c1 - c0], ACT.Copy).then_inc(turned_kept, 1)
            act.wait_ge(ln_var, 1)
            act.activation(rstd[0:T, :], rstd[0:T, :], ACT.Sqrt).then_inc(ln_std, 1)
            act.wait_ge(psq_ready, 1)
            act.activation(psq[:, 1:2], psq[:, 0:1], ACT.Sqrt).then_inc(pnorm_ready, 1)
            act.wait_ge(ln_ready, 1)
            with act.Fori(0, NT // 5) as i:
                for j in range(5):
                    t = i * 5 + j
                    act.activation(h_sb[0:T, ds(t, 1), :].rearrange("p a f -> p (a f)"),
                                   x_sb[0:T, ds(t, 1), :].rearrange("p a f -> p (a f)"), ACT.Relu,
                                   bias=nbias[0:T, ds(t, 1)], scale=rstd[0:T, ds(t, 1)]).then_inc(h_ready, 1)
            act.wait_ge(deg_ready, 1)
            act.activation(dtmp[0:T, 2, :], dtmp[0:T, 1, :], ACT.Sqrt).then_inc(deg_root, 1)
            act.wait_ge(dinv_ready, 1)
            act.wait_ge(h_ready, NT)
            for t in range(NT):
                act.activation(hp[0:T, t, :], h_sb[0:T, t, :], ACT.Copy, scale=dinv[0:T, t:t + 1]).then_inc(hp_ready, 1)
            for t in range(NT):
                act.wait_ge(hp_turned, t + 1)
                act.activation(acc[:, :, T * t:T * (t + 1)],
                               bank[2 + t % 4][:, 0:H * T].rearrange("p (h n) -> p h n", h=H),
                               ACT.Copy).then_inc(acc_init, 1)
            def stage_first(L, table):
                for v in range(WPI):
                    act.activation(idx_now[:, v, :], table[:, :, v], ACT.Copy).then_inc(idx_ready[L], 1)

            def stage_next(L, table, w, i):
                for v in range(WPI):
                    act.wait_ge(win_summed[L], (w * NIT + i) * WPI + (v + 1))
                    act.sem_inc(gate_a, 1)
                    act.activation(idx_now[:, v, :],
                                   table[:, :, ds(i * WPI + (WPI + v), 1)].rearrange("p k a -> p (k a)"),
                                   ACT.Copy).then_inc(idx_ready[L], 1)

            def stage_more(L, table, n_pass):
                with act.If(n_pass > 1):
                    with act.Fori(1, n_pass) as w:
                        with act.Fori(0, NIT) as i:
                            stage_next(L, table, w, i)
                act.sem_inc(gate_a, 1)

            def take_tile(t):
                act.wait_ge(tile_mul, t + 1)
                act.sem_inc(gate_a, 1)
                act.activation(s_tile[:, 0, :, :], acc[:, :, ds(t * T, T)], ACT.Copy).then_inc(tile_in, 1)

            def norm_tile(t):
                act.wait_ge(t_var, t + 1)
                act.sem_inc(gate_a, 1)
                act.activation(ln[0:T, 9:10], ln[0:T, 8:9], ACT.Sqrt).then_inc(t_std, 1)
                act.wait_ge(t_ln, t + 1)
                act.wait_ge(h2_turned, t + 1)
                act.sem_inc(gate_a, 1)
                act.activation(h2[0:T, :], x_sb[0:T, ds(t, 1), :].rearrange("p a f -> p (a f)"), ACT.Relu,
                               bias=ln[0:T, 11:12], scale=ln[0:T, 10:11]).then_inc(h2_ready, 1)

            def keep_tile(t):
                act.wait_ge(h2_turned, t + 2)
                act.sem_inc(gate_a, 1)
                act.activation(h2_t[:, :, :], bank[5][:, 0:H * T].rearrange("p (h n) -> p h n", h=H),
                               ACT.Copy).then_inc(h2_kept, 1)
                for q in range(2):
                    act.wait_ge(prod_ready, t * 4 + (2 * q + 1))
                    act.wait_ge(rows_free[q], t + 1)
                    act.sem_inc(gate_a, 1)
                    act.activation(rows2[0:T, 2 * q, :], bank[6][0:T, :], ACT.Copy).then_inc(prod_kept_a, 1)

            act.sem_inc(h2_ready, 1)
            act.sem_inc(prod_kept_a, 1)
            act.wait_ge(passes_ready, 1)
            n_pass = act.value_load(passes[0:1, 0:1], min_val=1, max_val=NPASS)
            act.wait_ge(a_step, 2)
            stage_first(0, src_t)
            act.wait_ge(score_ready, 1)
            act.activation(th[0:T, :], score[0:T, 1, :], ACT.Tanh).then_inc(tanh_ready, 1)
            for i in range(FIRST_IT):
                stage_next(0, src_t, 0, i)
            for m in range(H):
                act.wait_ge(gates_ready, 2 * m + 1)
                act.activation(rz[:, m, :], bank[4 + m][:, :], ACT.Sigmoid).then_inc(rz_ready, 1)
            for m in range(H):
                act.wait_ge(cand_in, m + 1)
                act.activation(cand[:, m, :], gtmp[:, m, :], ACT.Tanh).then_inc(cand_ready, 1)
            act.wait_ge(cand_ready, 2)
            act.wait_ge(w_ready, 2)
            with act.Fori(FIRST_IT, NIT) as i:
                t = i - FIRST_IT
                take = act.value_load(early_i[0:1, ds(i, 1)], min_val=0, max_val=1)
                with act.If(take > 0):
                    act.wait_ge(win_added[0], i * WPI)
                    act.sem_inc(gate_a, 1)
                    take_tile(t)
                    norm_tile(t)
                stage_next(0, src_t, 0, i)
                with act.If(take > 0):
                    keep_tile(t)
                act.sem_inc(gate_a, 1)
            stage_more(0, src_t, n_pass)
            t0 = act.value_load(passes[0:1, 1:2], min_val=0, max_val=NT - 2)
            act.wait_ge(agg_done[0], 1)
            take_tile(t0)
            norm_tile(t0)
            with act.Fori(t0, NT - 1) as t:
                take_tile(t + 1)
                keep_tile(t)
                norm_tile(t + 1)
            keep_tile(NT - 1)

            stage_first(1, idx2_t)
            with act.Fori(0, NIT) as i:
                stage_next(1, idx2_t, 0, i)
            stage_more(1, idx2_t, n_pass)
            act.wait_ge(bn_var, 1)
            act.activation(bn[:, :, 3], bn[:, :, 2], ACT.Sqrt).then_inc(bn_std, 1)
            act.wait_ge(bn_ready, 1)
            with act.Fori(0, NT // 5) as i:
                for j in range(5):
                    act.wait_ge(fin_turned, i * 5 + (j + 1))
                    act.sem_inc(gate_a, 1)
                    for h in range(H):
                        last = act.activation(s_tile[:, j, h, :], acc[:, h, ds(i * (5 * T) + j * T, T)], ACT.Identity,
                                              bias=bn[:, h, 6:7], scale=bn[:, h, 5:6])
                    last.then_inc(fin_in, 1)

        @block.vector
        def _(dve):
            n = [0]

            def step(ins):
                n[0] += 1
                ins.then_inc(d_step, 1)
                dve.wait_ge(d_step, n[0])

            dve.wait_ge(edges_in, EDGE_DMAS)
            step(dve.tensor_copy(dst_f, dst_i))
            dve.tensor_reduce(span[0:NG, 0:1], dst_f, AX.X, ALU.min)
            step(dve.tensor_reduce(span[0:NG, 1:2], dst_f, AX.X, ALU.max))
            dve.tensor_scalar(rel_g, dst_f, span[0:NG, 0:1], None, ALU.subtract).then_inc(edges_ready, 1)
            step(dve.tensor_tensor(span[0:NG, 2:3], span[0:NG, 1:2], span[0:NG, 0:1], ALU.subtract))
            step(dve.tensor_scalar(hi_g, dst_f, 1.0 / T, 0.5 / T - 0.5, ALU.mult, ALU.add))
            step(dve.tensor_scalar(hi_g, hi_g, MAGIC, MAGIC, ALU.add, ALU.subtract))
            step(dve.scalar_tensor_tensor(lo_g, hi_g, -float(T), dst_f, ALU.mult, ALU.add))
            step(dve.tensor_copy(src_g, src_i))
            dve.scalar_tensor_tensor(idx2_g, src_i, float(NREL), rel_i, ALU.mult, ALU.add).then_inc(edges_ready, 1)

            dve.wait_ge(x_in, 32)
            base = n[0]
            with dve.Fori(0, NT // 5) as i:
                for j in range(5):
                    t = i * 5 + j
                    dve.bn_stats(st6[0:T, ds(t, 1), :].rearrange("p a f -> p (a f)"),
                                 x_sb[0:T, ds(t, 1), :].rearrange("p a f -> p (a f)")).then_inc(d_step, 1)
            n[0] += NT
            dve.wait_ge(d_step, n[0])
            for t in range(NT):
                last = dve.bn_aggr(mv[0:T, t, :], st6[0:T, t, :])
            step(last)
            dve.tensor_scalar(rstd[0:T, :], mv[0:T, :, 1], EPS, None, ALU.add).then_inc(ln_var, 1)
            dve.wait_ge(pool_in, 16)
            dve.tensor_tensor_reduce(out=oh_rank[:, 0, :], in0=pbc[:, :], in1=pbc[:, :], scale=1.0, scalar=0.0,
                                     op0=ALU.mult, op1=ALU.add, accum_out=psq[:, 0:1]).then_inc(psq_ready, 1)
            dve.wait_ge(ln_std, 1)
            step(dve.reciprocal(rstd[0:T, :], rstd[0:T, :]))
            dve.scalar_tensor_tensor(nbias[0:T, :], mv[0:T, :, 0], -1.0, rstd[0:T, :], ALU.mult,
                                     ALU.mult).then_inc(ln_ready, 1)

            dve.wait_ge(edges_turned, 2)
            dve.tensor_copy(lo_t[:, :], bank[0][:, 0:BPW * NG])
            dve.tensor_copy(hi_t[:, :], bank[1][:, 0:BPW * NG]).then_inc(edges_kept_d, 1)
            dve.wait_ge(edges_turned, 7)
            dve.wait_ge(consts, 8)
            dve.tensor_copy(base_row[:, 0, :], bank[6][0:1, 0:NG])
            step(dve.tensor_copy(base_row[:, 1, :], bank[6][0:1, 0:NG]))
            dve.tensor_copy(base_i[:, :], base_row[:, 0, :])
            step(dve.tensor_reduce(flag[:, 0:1], bank[6][0:1, P:P + NG], AX.X, ALU.max))
            step(dve.tensor_scalar(flag[:, 1:2], flag[:, 0:1], 1.0 / W, 0.5 / W - 0.5, ALU.mult, ALU.add))
            step(dve.tensor_scalar(flag[:, 1:2], flag[:, 1:2], MAGIC, MAGIC, ALU.add, ALU.subtract))
            dve.tensor_scalar(passes[:, 0:1], flag[:, 1:2], 1.0, None, ALU.add)
            step(dve.tensor_scalar(flag[:, 2:3], flag[:, 1:2], 0.5, None, ALU.is_lt))
            step(dve.memset(least[:, :, :], 1e9))
            step(dve.tensor_reduce(least[:, 0, 0:NIT], base_row[:, 0, :].rearrange("p (i v) -> p i v", v=WPI),
                                   AX.X, ALU.min))
            for q, d in enumerate((1, 2, 4, 8, 16)):
                step(dve.tensor_tensor(least[:, 1 - q % 2, 0:NIT], least[:, q % 2, 0:NIT], least[:, q % 2, d:NIT + d],
                                       ALU.min))
            step(dve.tensor_scalar(early[:, 0, :], iota[0:1, 0:NIT], float(T), float(T * (1 - FIRST_IT)),
                                   ALU.mult, ALU.add))
            step(dve.tensor_tensor(early[:, 1, :], least[:, 1, 0:NIT], early[:, 0, :], ALU.is_ge))
            step(dve.tensor_tensor_scan(early[:, 2, :], early[:, 1, :], zrow[0:1, 0:NIT], flag[:, 2:3],
                                        ALU.mult, ALU.add))
            step(dve.tensor_reduce(flag[:, 3:4], early[:, 2, FIRST_IT:NIT], AX.X, ALU.add))
            dve.tensor_copy(early_i[:, :], early[:, 2, :])
            dve.tensor_copy(passes[:, 1:2], flag[:, 3:4]).then_inc(passes_ready, 1)

            dve.wait_ge(turned_kept, 2)
            ewf = ew_t[:, :, :].rearrange("p k g -> p (k g)")
            step(dve.tensor_copy(ewp[:, 0, :], ewf))
            step(dve.tensor_tensor(ew_r[:, 0, :], ewf, ewp[:, 0, :], ALU.subtract))
            step(dve.tensor_copy(ewp[:, 1, :], ew_r[:, 0, :]))
            step(dve.tensor_tensor(ew_r[:, 1, :], ew_r[:, 0, :], ewp[:, 1, :], ALU.subtract))
            step(dve.tensor_copy(ewp[:, 2, :], ew_r[:, 1, :]))

            dve.wait_ge(edges_kept_d, 1)
            base = n[0]
            with dve.Fori(0, NCH // 2) as i:
                for b in range(2):
                    c = i * (2 * CB) + b * CB
                    dve.wait_ge(chunk_summed, i * 2 + (b + 1))
                    dve.sem_inc(gate_d, 1)
                    dve.tensor_tensor(oh_hi[b], iota_rep[:, 0:NT, :],
                                      hi_t[:, ds(c, CB)].unsqueeze(1).broadcast_to([P, NT, CB]),
                                      ALU.is_equal).then_inc(d_step, 1)
                    dve.tensor_tensor(oh_lo[b], iota_rep, lo_t[:, ds(c, CB)].unsqueeze(1).broadcast_to([P, T, CB]),
                                      ALU.is_equal)
                    dve.wait_ge(d_step, i * 2 + (base + b + 1))
                    for s in range(3):
                        last = dve.tensor_tensor(oh_ew[b][:, s, :, :], oh_hi[b],
                                                 ewp[:, s, ds(c, CB)].unsqueeze(1).broadcast_to([P, NT, CB]), ALU.mult)
                    last.then_inc(chunk_ready, 1)
            n[0] += NCH
            dve.wait_ge(deg_summed, 1)
            step(dve.tensor_copy(degs[0:T, :], bank[0][0:T, 0:3 * NT]))
            step(dve.tensor_tensor(dtmp[0:T, 0, :], degs[0:T, NT:2 * NT], degs[0:T, 2 * NT:3 * NT], ALU.add))
            step(dve.tensor_tensor(dtmp[0:T, 0, :], dtmp[0:T, 0, :], degs[0:T, 0:NT], ALU.add))
            step(dve.tensor_scalar(dtmp[0:T, 0, :], dtmp[0:T, 0, :], 1.0, None, ALU.add))
            step(dve.tensor_scalar(dtmp[0:T, 3, :], dtmp[0:T, 0, :], 0.0, None, ALU.is_gt))
            dve.tensor_scalar(dtmp[0:T, 1, :], dtmp[0:T, 0, :], 1e-30, None, ALU.max).then_inc(deg_ready, 1)
            dve.wait_ge(deg_root, 1)
            step(dve.reciprocal(dinv[0:T, :], dtmp[0:T, 2, :]))
            dve.tensor_tensor(dinv[0:T, :], dinv[0:T, :], dtmp[0:T, 3, :], ALU.mult).then_inc(dinv_ready, 1)

            dve.wait_ge(h_ready, NT)
            base = n[0]
            for t in range(NT):
                if t >= 3:
                    dve.wait_ge(d_step, base + t - 2)
                last = dve.tensor_tensor_reduce(out=oh_rank[0:T, 1 + t % 3, :], in0=h_sb[0:T, t, :], in1=pbc[0:T, :],
                                                scale=1.0, scalar=0.0, op0=ALU.mult, op1=ALU.add,
                                                accum_out=score[0:T, 0, t:t + 1]).then_inc(d_step, 1)
            n[0] += NT
            dve.wait_ge(d_step, n[0])
            dve.wait_ge(pnorm_ready, 1)
            step(dve.reciprocal(psq[:, 2:3], psq[:, 1:2]))
            dve.tensor_scalar(score[0:T, 1, :], score[0:T, 0, :], psq[0:T, 2:3], None, ALU.mult).then_inc(score_ready, 1)
            dve.wait_ge(score_turned, 1)
            dve.tensor_copy(score_t[:, :], bank[5][0:NT, 0:T]).then_inc(score_kept, 1)
            step(dve.memset(cnt[0:T, :, :], 0.0))
            step(dve.memset(outdone[0:T, :], 0.0))

            def hot(L, i, v):
                g = i * WPI + v
                if L == 0:
                    for k in range(BPW):
                        last = dve.tensor_scalar(onehot[:, v, k, :], iota_w[:, :], rel_t[:, k, ds(g, 1)],
                                                 ew_t[:, k, ds(g, 1)], ALU.is_equal, ALU.mult)
                else:
                    last = dve.tensor_tensor(onehot[:, v, :, :], iota_w[:, :].unsqueeze(1).broadcast_to([P, BPW, W]),
                                             rel_t[:, :, ds(g, 1)].broadcast_to([P, BPW, W]), ALU.is_equal)
                last.then_inc(hot_ready[L], 1)

            def hots(L, i):
                for v in range(WPI):
                    hot(L, i, v)

            def adds(L, w, i):
                base = [dve.value_load(base_i[0:1, ds(i * WPI + v, 1)], min_val=0, max_val=N) for v in range(WPI)]
                for v in range(WPI):
                    at = acc[:, :, ds(base[v], W)]
                    dve.wait_ge(win_summed[L], (w * NIT + i) * WPI + (v + 1))
                    dve.tensor_tensor(at, at, win[v], ALU.add).then_inc(win_added[L], 1)
                    dve.wait_ge(win_added[L], (w * NIT + i) * WPI + (v + 1))

            def more_passes(L, n_pass):
                with dve.If(n_pass > 1):
                    with dve.Fori(1, n_pass) as w:
                        dve.tensor_scalar(iota_w[:, :], iota_w[:, :], float(W), None, ALU.add).then_inc(pass_step[L], 1)
                        dve.tensor_scalar(base_row[:, 1, :], base_row[:, 1, :], float(W), float(N), ALU.add,
                                          ALU.min).then_inc(pass_step[L], 1)
                        dve.wait_ge(pass_step[L], w * 3 - 1)
                        dve.sem_inc(gate_d, 1)
                        dve.tensor_copy(base_i[:, :], base_row[:, 1, :]).then_inc(pass_step[L], 1)
                        dve.wait_ge(pass_step[L], w * 3)
                        dve.sem_inc(gate_d, 1)
                        with dve.Fori(0, NIT) as i:
                            hots(L, i)
                            adds(L, w, i)
                dve.sem_inc(gate_d, 1)

            def compare_tile(t):
                s = score[0:T, 1, t:t + 1]
                if t < NT - 1:
                    if t >= 2:
                        dve.wait_ge(mask_used, t - 1)
                    dve.tensor_scalar(mask[t % 2][0:T, 0:N - T * (t + 1)], s_all[:, T * (t + 1):N], s, 0.0,
                                      ALU.is_gt, ALU.add, accum_out=cnt[0:T, t, 0:1]).then_inc(mask_ready, 1)
                step(dve.tensor_scalar(cmp_out[0:T, 0, :], s_all[:, T * t:T * (t + 1)], s, 0.0, ALU.is_gt, ALU.add,
                                       accum_out=cnt[0:T, t, 1:2]))
                step(dve.scalar_tensor_tensor(cmp_out[0:T, 1, :], s_all[:, T * t:T * (t + 1)], s, lower[0:T, :],
                                              ALU.is_equal, ALU.mult, accum_out=cnt[0:T, t, 2:3]))

            def add_counts(t):
                dve.wait_ge(mask_used, t + 1)
                if t:
                    dve.wait_ge(counts_added, t)
                dve.tensor_tensor(outdone[0:T, t + 1:NT], outdone[0:T, t + 1:NT], beaten[t % 2][:, t + 1:NT],
                                  ALU.add).then_inc(counts_added, 1)

            def rank_tiles(a, b):
                step(dve.tensor_reduce(rtmp[0:T, 0, a:b], cnt[0:T, a:b, :], AX.X, ALU.add))
                step(dve.tensor_tensor(rtmp[0:T, 1, a:b], rtmp[0:T, 0, a:b], outdone[0:T, a:b], ALU.subtract))
                step(dve.scalar_tensor_tensor(rank[0:T, a:b], iota[0:T, a:b], float(T), rtmp[0:T, 1, a:b],
                                              ALU.mult, ALU.add))
                dve.wait_ge(tanh_ready, 1)
                for t in range(a, b):
                    if t >= 4:
                        dve.wait_ge(rank_used, t - 3)
                    dve.tensor_scalar(oh_rank[0:T, t % 4, :], iota[0:T, :], rank[0:T, t:t + 1], th[0:T, t:t + 1],
                                      ALU.is_equal, ALU.mult).then_inc(rank_hot, 1)

            n_pass = dve.value_load(passes[0:1, 0:1], min_val=1, max_val=NPASS)
            step(dve.tensor_copy(iota_w[:, :], iota[:, 0:W]))
            for i, quarters in enumerate(RANKED):
                hots(0, i)
                if i == 0:
                    dve.wait_ge(scores_in, 32)
                    dve.wait_ge(acc_init, NT)
                for tiles in quarters:
                    for t in tiles:
                        compare_tile(t)
                        if t != tiles[0] or tiles != quarters[0]:
                            if t < NT - 1:
                                add_counts(t - 1)
                adds(0, 0, i)
                add_counts(min(t, NT - 2))
                dve.wait_ge(counts_added, min(t, NT - 2) + 1)
                rank_tiles(quarters[0][0], quarters[-1][-1] + 1)
            hots(0, GRU_IT)
            dve.wait_ge(rank_used, NT)
            dve.tensor_copy(xt[:, 0, :], bank[6][:, 0:F]).then_inc(xt_kept, 1)
            dve.tensor_copy(xt[:, 1, :], bank[7][:, 0:F]).then_inc(xt_kept, 1)
            adds(0, 0, GRU_IT)
            for m in range(H):
                dve.wait_ge(rz_ready, m + 1)
                dve.wait_ge(gates_ready, 2 * m + 2)
                step(dve.tensor_tensor(gtmp[:, m, :], rz[:, m, 0:F], bank[6 + m][:, F:2 * F], ALU.mult))
                dve.tensor_tensor(gtmp[:, m, :], gtmp[:, m, :], bank[6 + m][:, 0:F], ALU.add).then_inc(cand_in, 1)
            for m in range(H):
                dve.wait_ge(cand_ready, m + 1)
                step(dve.tensor_tensor(w_new[:, m, :], h0[:, m, :], cand[:, m, :], ALU.subtract))
                step(dve.tensor_tensor(w_new[:, m, :], w_new[:, m, :], rz[:, m, F:2 * F], ALU.mult))
                dve.tensor_tensor(w_new[:, m, :], w_new[:, m, :], cand[:, m, :], ALU.add).then_inc(w_ready, 1)

            def norm_tile(t):
                row = x_sb[0:T, ds(t, 1), :].rearrange("p a f -> p (a f)")
                dve.wait_ge(h2_ready, t + 1)
                dve.wait_ge(tile_mul, t + 2)
                dve.scalar_tensor_tensor(row, bank[4][0:T, 0:F], dinv[0:T, ds(t, 1)], row, ALU.mult,
                                         ALU.add).then_inc(t_step, 1)
                dve.wait_ge(t_step, t * 4 + 1)
                dve.sem_inc(gate_d, 1)
                dve.bn_stats(ln[0:T, 0:6], row).then_inc(t_step, 1)
                dve.wait_ge(t_step, t * 4 + 2)
                dve.sem_inc(gate_d, 1)
                dve.bn_aggr(ln[0:T, 6:8], ln[0:T, 0:6]).then_inc(t_step, 1)
                dve.wait_ge(t_step, t * 4 + 3)
                dve.tensor_scalar(ln[0:T, 8:9], ln[0:T, 7:8], EPS, None, ALU.add).then_inc(t_var, 1)
                dve.wait_ge(t_std, t + 1)
                dve.reciprocal(ln[0:T, 10:11], ln[0:T, 9:10]).then_inc(t_step, 1)
                dve.wait_ge(t_step, t * 4 + 4)
                dve.tensor_scalar(ln[0:T, 11:12], ln[0:T, 6:7], ln[0:T, 10:11], -1.0, ALU.mult, ALU.mult).then_inc(t_ln, 1)

            def keep_tile(t):
                for q in range(2):
                    dve.wait_ge(prod_ready, t * 4 + (2 * q + 2))
                    dve.wait_ge(rows_free[q], t + 1)
                    dve.sem_inc(gate_d, 1)
                    dve.tensor_copy(rows2[0:T, 2 * q + 1, :], bank[7][0:T, :]).then_inc(prod_kept_d, 1)

            dve.sem_inc(prod_kept_d, 1)
            with dve.Fori(FIRST_IT, NIT) as i:
                t = i - FIRST_IT
                take = dve.value_load(early_i[0:1, ds(i, 1)], min_val=0, max_val=1)
                hots(0, i)
                with dve.If(take > 0):
                    norm_tile(t)
                adds(0, 0, i)
                dve.sem_inc(gate_d, 1)
                with dve.If(take > 0):
                    keep_tile(t)
                dve.sem_inc(gate_d, 1)
            more_passes(0, n_pass)
            dve.sem_inc(agg_done[0], 1)
            t0 = dve.value_load(passes[0:1, 1:2], min_val=0, max_val=NT - 2)
            norm_tile(t0)
            with dve.Fori(t0, NT - 1) as t:
                norm_tile(t + 1)
                keep_tile(t)
            keep_tile(NT - 1)

            dve.wait_ge(cleared, 1)
            step(dve.tensor_copy(iota_w[:, :], iota[:, 0:W]))
            step(dve.tensor_copy(base_i[:, :], base_row[:, 0, :]))
            step(dve.tensor_copy(base_row[:, 1, :], base_row[:, 0, :]))
            with dve.Fori(0, NIT) as i:
                hots(1, i)
                adds(1, 0, i)
            more_passes(1, n_pass)
            CH = [(c, min(c + 512, N)) for c in range(0, N, 512)]
            for h in range(H):
                for q, (lo, hi) in enumerate(CH):
                    last = dve.bn_stats(bn6[:, h, q, :], acc[:, h, lo:hi])
            step(last)
            for h in range(H):
                last = dve.bn_aggr(bn[:, h, 0:2], bn6[:, h, :, :].rearrange("p q s -> p (q s)"))
            step(last)
            dve.tensor_scalar(bn[:, :, 2], bn[:, :, 1], EPS, None, ALU.add).then_inc(bn_var, 1)
            dve.wait_ge(bn_std, 1)
            dve.wait_ge(small_in, 96)
            step(dve.reciprocal(bn[:, :, 4], bn[:, :, 3]))
            step(dve.tensor_tensor(bn[:, :, 5], bn[:, :, 4], gb[:, 0, :], ALU.mult))
            step(dve.tensor_tensor(bn[:, :, 7], bn[:, :, 0], bn[:, :, 5], ALU.mult))
            dve.tensor_tensor(bn[:, :, 6], gb[:, 1, :], bn[:, :, 7], ALU.subtract).then_inc(bn_ready, 1)
            dve.sem_inc(fin_ready, 5)
            with dve.Fori(0, NT // 5) as i:
                for j in range(5):
                    row = x_sb[0:T, ds(i * 5 + j, 1), :].rearrange("p a f -> p (a f)")
                    dve.wait_ge(fin_turned, i * 5 + (j + 6))
                    dve.tensor_tensor(row, row, bank[j][0:T, 0:F], ALU.add).then_inc(fin_ready, 1)

        @block.tensor
        def _(pe):
            pe.wait_ge(consts, 8)
            pe.wait_ge(edges_ready, 2)
            pe.wait_ge(pads_ready, 2)
            for b, a in enumerate((lo_g, hi_g, rel_g, ew_g, src_g, idx2_g)):
                for k in range(BPW):
                    last = pe.transpose(bank[b][:, NG * k:NG * (k + 1)], a[:, P * k:P * (k + 1)], ident[0:NG, 0:NG])
                last.then_inc(edges_turned, 1)
            pe.transpose(bank[6][0:1, 0:NG], span[0:NG, 0:1], ident[0:NG, 0:NG])
            pe.transpose(bank[6][0:1, P:P + NG], span[0:NG, 2:3], ident[0:NG, 0:NG]).then_inc(edges_turned, 1)
            pe.wait_ge(gru_in, 48)
            for n in range(8):
                k, g = n // 4, n % 4
                pe.wait_ge(turned_kept, n + 1)
                for q in range(4 * g, min(4 * g + 4, 14)):
                    a = gru_raw[:, q, P * k:P * (k + 1)] if q < 12 else h0[:, q - 12, P * k:P * (k + 1)]
                    last = pe.transpose(bank[2 + n % 4][:, P * (q - 4 * g):P * (q - 4 * g + 1)], a, ident[:, :])
                last.then_inc(gru_turned, 1)
            pe.sem_inc(chunk_summed, 2)
            degree = bank[0][0:T, 0:3 * NT]
            pe.wait_ge(edges_kept_d, 1)
            pe.matmul(degree, ones[0:1, 0:T], zrow[0:1, 0:3 * NT], start=True, stop=False)
            with pe.Fori(0, NCH // 2) as i:
                for b in range(2):
                    pe.wait_ge(chunk_ready, i * 2 + (b + 1))
                    for c in range(CB):
                        last = pe.matmul(degree, oh_lo[b][:, :, c], oh_ew[b][:, :, :, c].rearrange("p s c -> p (s c)"),
                                         start=False, stop=False)
                    last.then_inc(chunk_summed, 1)
            pe.matmul(degree, ones[0:1, 0:T], zrow[0:1, 0:3 * NT], start=False, stop=True).then_inc(deg_summed, 1)
            for t in range(NT):
                pe.wait_ge(hp_ready, t + 1)
                pe.wait_ge(turned_kept, 12)
                if t >= 4:
                    pe.wait_ge(acc_init, t - 3)
                for h in range(H):
                    last = pe.transpose(bank[2 + t % 4][:, T * h:T * (h + 1)], hp[0:T, t, P * h:P * (h + 1)],
                                        ident[0:T, 0:T])
                last.then_inc(hp_turned, 1)
            pe.wait_ge(score_ready, 1)
            pe.wait_ge(acc_init, NT)
            pe.transpose(bank[5][0:NT, 0:T], score[0:T, 1, :], ident[0:T, 0:T]).then_inc(score_turned, 1)

            def sum_window(L, w, i, v):
                pe.wait_ge(hot_ready[L], (w * NIT + i) * WPI + (v + 1))
                pe.wait_ge(gathered[L][v], (w * NIT + i) * (16 * BPW) + 16 * BPW)
                for h in range(H):
                    for k in range(BPW):
                        last = pe.matmul(win[v][:, h, :], ring[:, BPW * v + k, P * h:P * (h + 1)],
                                         onehot[:, v, k, :], start=(k == 0), stop=(k == BPW - 1))
                last.then_inc(win_summed[L], 1)

            def sum_windows(L, w, i):
                for v in range(WPI):
                    sum_window(L, w, i, v)

            def sum_more(L, n_pass):
                with pe.If(n_pass > 1):
                    with pe.Fori(1, n_pass) as w:
                        with pe.Fori(0, NIT) as i:
                            sum_windows(L, w, i)
                pe.sem_inc(gate_pe, 1)

            def count_masks(t):
                pe.wait_ge(mask_ready, t + 1)
                if t >= 2:
                    pe.wait_ge(counts_added, t - 1)
                for u in range(t + 1, NT):
                    last = pe.matmul(beaten[t % 2][:, u:u + 1], mask[t % 2][0:T, T * (u - t - 1):T * (u - t)],
                                     ones_b[0:T, :], start=True, stop=True)
                last.then_inc(mask_used, 1)

            def pick_rows(a, b):
                for t in range(a, b):
                    pe.wait_ge(rank_hot, t + 1)
                    for h in range(H):
                        last = pe.matmul(bank[6 + h][:, 0:F], h_sb[0:T, t, P * h:P * (h + 1)], oh_rank[0:T, t % 4, :],
                                         start=(t == 0), stop=(t == NT - 1))
                    last.then_inc(rank_used, 1)

            pe.sem_inc(tile_mul, 1)
            pe.sem_inc(h2_turned, 1)
            pe.wait_ge(passes_ready, 1)
            n_pass = pe.value_load(passes[0:1, 0:1], min_val=1, max_val=NPASS)
            pe.wait_ge(score_kept, 1)
            for i, quarters in enumerate(RANKED):
                if i:
                    pick_rows(RANKED[i - 1][0][0], quarters[0][0])
                for v, tiles in enumerate(quarters):
                    sum_window(0, 0, i, v)
                    for t in tiles:
                        if t < NT - 1:
                            count_masks(t)
            pick_rows(RANKED[-1][0][0], NT)
            sum_windows(0, 0, GRU_IT)
            pe.wait_ge(xt_kept, 2)
            pe.wait_ge(small_in, 96)
            for m in range(H):
                xs = [xt[:, k, P * m:P * (m + 1)] for k in range(H)]
                hs = [gru_t[:, k, 12 * P + P * m:12 * P + P * (m + 1)] for k in range(H)]
                for k in range(H):
                    pe.matmul(bank[4 + m][:, :], xs[k], gru_t[:, k, 0:2 * F], start=(k == 0), stop=False)
                    pe.matmul(bank[4 + m][:, :], hs[k], gru_t[:, k, 3 * F:5 * F], start=False, stop=False)
                pe.matmul(bank[4 + m][:, :], ones[:, :], brow[:, 0, 0:2 * F], start=False, stop=False)
                pe.matmul(bank[4 + m][:, :], ones[:, :], brow[:, 1, 0:2 * F], start=False, stop=True).then_inc(gates_ready, 1)
                for q, (a, c) in enumerate(((xs, 2 * F), (hs, 5 * F))):
                    o = bank[6 + m][:, F * q:F * (q + 1)]
                    for k in range(H):
                        pe.matmul(o, a[k], gru_t[:, k, c:c + F], start=(k == 0), stop=False)
                    last = pe.matmul(o, ones[:, :], brow[:, q, 2 * F:3 * F], start=False, stop=True)
                last.then_inc(gates_ready, 1)
            pe.wait_ge(w_ready, 2)
            pe.wait_ge(wrel_in, 32)

            def times_w(t):
                pe.wait_ge(tile_in, t + 1)
                for h in range(H):
                    last = pe.matmul(bank[4][0:T, 0:F], s_tile[:, 0, h, :], w_new[:, h, :],
                                     start=(h == 0), stop=(h == H - 1))
                last.then_inc(tile_mul, 1)

            def turn_h2(t):
                pe.wait_ge(h2_ready, t + 2)
                for h in range(H):
                    last = pe.transpose(bank[5][:, T * h:T * (h + 1)], h2[0:T, P * h:P * (h + 1)], ident[0:T, 0:T])
                last.then_inc(h2_turned, 1)

            def products(t):
                pe.wait_ge(h2_kept, t + 1)
                for q in range(4):
                    pe.wait_ge(prod_kept_a if q % 2 == 0 else prod_kept_d, t * 2 + (q // 2 + 1))
                    for k in range(H):
                        last = pe.matmul(bank[6 + q % 2][0:T, :], h2_t[:, k, :], wr[:, k, 512 * q:512 * (q + 1)],
                                         start=(k == 0), stop=(k == H - 1))
                    last.then_inc(prod_ready, 1)

            with pe.Fori(FIRST_IT, NIT) as i:
                t = i - FIRST_IT
                take = pe.value_load(early_i[0:1, ds(i, 1)], min_val=0, max_val=1)
                with pe.If(take > 0):
                    times_w(t)
                sum_windows(0, 0, i)
                with pe.If(take > 0):
                    turn_h2(t)
                    products(t)
                pe.sem_inc(gate_pe, 1)
            sum_more(0, n_pass)
            t0 = pe.value_load(passes[0:1, 1:2], min_val=0, max_val=NT - 2)
            times_w(t0)
            with pe.Fori(t0, NT - 1) as t:
                turn_h2(t)
                times_w(t + 1)
                products(t)
            turn_h2(NT - 1)
            products(NT - 1)

            with pe.Fori(0, NIT) as i:
                sum_windows(1, 0, i)
            sum_more(1, n_pass)
            pe.sem_inc(fin_turned, 5)
            with pe.Fori(0, NT // 5) as i:
                for j in range(5):
                    pe.wait_ge(fin_in, i * 5 + (j + 1))
                    pe.wait_ge(fin_ready, i * 5 + (j + 1))
                    for h in range(H):
                        last = pe.transpose(bank[j][0:T, P * h:P * (h + 1)], s_tile[:, j, h, :], ident[:, :])
                    last.then_inc(fin_turned, 1)


_INS = ['x', 'src', 'dst', 'edge_type_8', 'edge_weight', 'L0_gnn_initial_weight', 'L0_gnn_pool_p', 'L0_gnn_gru_W_ih',
        'L0_gnn_gru_W_hh', 'L0_gnn_gru_b_ih', 'L0_gnn_gru_b_hh', 'L1_gnn_weight', 'L1_gnn_gamma', 'L1_gnn_beta']
_OUTS = [((N, F), 'float32')]


def kernel(**inputs):
    import numpy as _np
    import concourse.bacc as _bacc
    from concourse import mybir as _mybir
    from concourse.bass_utils import run_bass_kernel_spmd as _run

    nc = _bacc.Bacc("TRN2", target_bir_lowering=False, num_devices=1)
    arrays, args = {}, []
    for name in _INS:
        a = _np.ascontiguousarray(inputs[name])
        arrays[f"in_{name}_dram"] = a
        args.append(nc.dram_tensor(f"in_{name}_dram", a.shape, _mybir.dt.from_np(a.dtype), kind="ExternalInput").ap())
    for i, (shape, dtype) in enumerate(_OUTS):
        dt = _mybir.dt.from_np(_np.dtype(dtype))
        args.append(nc.dram_tensor(f"out_{i}_dram", shape, dt, kind="ExternalOutput").ap())
    gnn_kernel(nc, *args)
    r = _run(nc, [arrays], core_ids=[0])
    return r.results[0]["out_0_dram"]
```

```python
import concourse.bass as bass
from concourse import mybir
from contextlib import ExitStack

N, F, E = 3125, 256, 53125
NREL = 8
P = 128
H = F // P
T = 125
NT = N // T
BPW = 4
EW = BPW * P
W = 40
NG = -(-E // EW)
WPI = 4
NIT = NG // WPI
NPASS = -(-N // W)
APAD = N + 75
SLOTS = WPI * BPW
HC = NT + 1
EPS = 1e-5
COMPARED_FIRST = [0, 1]
COMPARED = [[t] for t in range(2, 14)] + [[14, 15], [16, 17], [18, 19], [20, 21], [22, 23], [24]]
RANKED = {1: (0, 4), 5: (4, 8), 9: (8, 12), 13: (12, 17), 15: (17, 21), 17: (21, NT)}
HOT_RANKS = {1: [0, 1], 2: [2, 3], 5: [4, 5], 6: [6, 7], 9: [8, 9], 10: [10, 11], 13: [12, 13, 14], 14: [15, 16],
             15: [17, 18, 19], 16: [20], 17: [21, 22, 23], 18: [24]}
GRU_IT = 5
FIRST_IT = GRU_IT + 1
TURNS = [(0, 4), (4, 7), (7, 10), (10, 13), (13, 16)]
GIT, GT = 4, len(TURNS)
GROUPS = 4
SINGLE_IT = FIRST_IT + GROUPS * GIT
EARLY = GROUPS * GT + NIT - SINGLE_IT
LAG = SINGLE_IT - GROUPS * GT
CUTS = [0, 4, 8, 12, 16, 20, NT]
PAIRS = [(t, min(t + 2, NT)) for t in range(0, NT, 2)]
MAGIC = 1.5 * 2 ** 23
IOTA = W - 1 + 2 * T
FULL, LAST = NG - 1, E - (NG - 1) * EW
SPLIT = [(0, 112), (112, T)]
assert NT * T == N and NIT * WPI == NG and NG <= P and W < T and EARLY < NT


def gnn_kernel(nc, x, src, dst, rel, ew, w0, pool_p, wih, whh, bih, bhh, wrel, gamma, beta, out):
    f32, bf16, i32 = mybir.dt.float32, mybir.dt.bfloat16, mybir.dt.int32
    ALU, ACT, AX = mybir.AluOpType, mybir.ActivationFunctionType, mybir.AxisListType
    ds = bass.ds

    table1 = nc.dram_tensor("table1", (N, F), f32, kind="Internal").ap()
    table2 = nc.dram_tensor("table2", (N, NREL * F), f32, kind="Internal").ap()
    score_row = nc.dram_tensor("score_row", (NT, T), f32, kind="Internal").ap()
    table2_rows = table2.rearrange("n (r f) -> (n r) f", r=NREL)

    with ExitStack() as ctx:
        def sb(name, shape, dt):
            return ctx.enter_context(nc.sbuf_tensor(name, shape, dt))

        def sem(name):
            return ctx.enter_context(nc.semaphore(name))

        x_sb = sb("x_sb", [P, NT, F], f32)
        h_sb = sb("h_sb", [P, NT, F], f32)
        acc = sb("acc", [P, H, APAD], f32)
        ring = sb("ring", [P, SLOTS, F], f32)
        onehot = sb("onehot", [P, WPI, BPW, W], f32)
        hot_tmp = sb("hot_tmp", [P, 2, BPW, W], f32)
        rel_neg = sb("rel_neg", [P, BPW, FIRST_IT * WPI], f32)
        iota_w0 = sb("iota_w0", [P, W], f32)
        idx_now = sb("idx_now", [P, WPI, BPW], i32)
        scr_a = sb("scr_a", [P, 8000], f32)
        scr_b = sb("scr_b", [P, 5120], f32)
        gru_t = sb("gru_t", [P, H, 14 * P], f32)
        rel_t = sb("rel_t", [P, BPW, NG + WPI], f32)
        ew_t = sb("ew_t", [P, BPW, NG + WPI], f32)
        src_t = sb("src_t", [P, BPW, NG + WPI], i32)
        idx2_t = sb("idx2_t", [P, BPW, NG + WPI], i32)
        rel_b = sb("rel_b", [P, BPW, NG], bf16)
        ewp = sb("ewp", [P, 3, BPW * NG], bf16)
        ew_r = sb("ew_r", [P, 2, BPW * NG], f32)
        iota = sb("iota", [P, IOTA], f32)
        iota_i = sb("iota_i", [P, IOTA], i32)
        iota_w = sb("iota_w", [P, W], f32)
        ident = sb("ident", [P, P], f32)
        lower = sb("lower", [P, T], f32)
        ones = sb("ones", [1, P], f32)
        span = sb("span", [P, 4], f32)
        base_row = sb("base_row", [1, 2, NG], f32)
        base_i = sb("base_i", [1, NG], i32)
        flag = sb("flag", [1, 4], f32)
        passes = sb("passes", [1, 3], i32)
        least = sb("least", [1, 2, NIT + 16], f32)
        early = sb("early", [1, 4, EARLY], f32)
        taken = sb("taken", [1, GROUPS, 8], i32)
        taken_one = sb("taken_one", [1, EARLY - GROUPS * GT, 4], i32)
        zrow = sb("zrow", [1, 3 * NG], f32)
        ones_b = sb("ones_b", [P, 1], bf16)
        cmp_out = sb("cmp_out", [P, 2, T], bf16)
        rtmp = sb("rtmp", [P, 2, NT], f32)
        outdone = sb("outdone", [P, NT], f32)
        mv = sb("mv", [P, NT, 2], f32)
        st6 = sb("st6", [P, NT, 6], f32)
        rstd = sb("rstd", [P, NT], f32)
        nbias = sb("nbias", [P, NT], f32)
        shift = sb("shift", [P, 2], f32)
        where = sb("where", [P, 4], f32)
        deg = sb("deg", [P, NT], f32)
        dinv = sb("dinv", [P, NT], f32)
        dtmp = sb("dtmp", [P, 4, NT], f32)
        pbc = sb("pbc", [P, F], f32)
        psq = sb("psq", [P, 4], f32)
        score = sb("score", [P, 2, NT], f32)
        score_t = sb("score_t", [NT, T], f32)
        cnt = sb("cnt", [P, NT, 2], f32)
        rank = sb("rank", [P, NT], f32)
        th = sb("th", [P, NT], f32)
        oh_rank = sb("oh_rank", [P, 4, F], f32)
        h0 = sb("h0", [P, H, F], f32)
        w_new = sb("w_new", [P, H, F], f32)
        brow = sb("brow", [1, 2, 3 * F], f32)
        h2 = sb("h2", [P, F], f32)
        h2_t = sb("h2_t", [P, H, T], f32)
        ln = sb("ln", [P, 12], f32)
        gb = sb("gb", [P, 2, H], f32)
        bn6 = sb("bn6", [P, H, NT, 6], f32)
        bn = sb("bn", [P, H, 8], f32)

        gh = gru_t[:, :, 3 * F:6 * F]
        gru_raw = ring[:, :, :].rearrange("p s f -> p (s f)")[:, 0:12 * F].rearrange("p (a f) -> p a f", a=12)
        A16 = scr_a[:, :].bitcast(bf16)
        iota_rep, oh_b0, oh_b1 = (A16[:, W * NG * i:W * NG * (i + 1)].rearrange("p (w g) -> p w g", g=NG)
                                  for i in range(3))
        oh_b = [oh_b0, oh_b1]
        spread = acc[0:NG, 0, 0:3 * W * HC // 2].bitcast(bf16).rearrange("p (s w c) -> p s w c", s=3, c=HC)
        base_lo = acc[0:NG, 1, 0:400].bitcast(bf16)[:, 0:IOTA]
        base_hi = acc[0:NG, 1, 400:500].bitcast(bf16)[:, 0:HC]
        degs = acc[0:W, 1, 500:500 + 3 * NG]
        deg_w = acc[0:W, 1, 900:900 + NG]
        deg_g = acc[0:NG, 1, 1100:1100 + 2 * W].rearrange("p (s w) -> p s w", s=2)
        deg_p = acc[0:NG, 1, 1200:1300].bitcast(bf16)[:, 0:3 * W].rearrange("p (s w) -> p s w", s=3)
        hp = scr_a[:, 0:NT * F].rearrange("p (t f) -> p t f", t=NT)
        wr = scr_a[:, 0:H * NREL * F].rearrange("p (k n) -> p k n", k=H)

        def ebuf(i):
            return scr_b[0:NG, EW * i:EW * (i + 1)]
        dst_i, src_i, rel_i = (ebuf(i).bitcast(i32) for i in range(3))
        ew_g, dst_f, rel_g, src_g, idx2_g = (ebuf(i) for i in range(3, 8))
        s_all = scr_b[0:T, 0:N]
        mask = [scr_b[:, N + 3:5120].bitcast(bf16), scr_a[:, NT * F:8000].bitcast(bf16)]
        def gbuf(i, n):
            return scr_b[:, H * F * i:H * F * (i + n)].rearrange("p (m f) -> p m f", m=H)
        xt, rz, cand, gtmp = gbuf(0, 1), gbuf(1, 2), gbuf(3, 1), gbuf(4, 1)
        s_tile = scr_b[:, 2048:2048 + H * T].rearrange("p (h n) -> p h n", h=H)
        rows2 = scr_b[:, 0:4 * 512].rearrange("p (c n) -> p c n", c=4)

        bank = [ctx.enter_context(nc.psum_tensor(f"bank{i}", [P, 512], f32)) for i in range(8)]
        win = [bank[v][:, 0:H * W].rearrange("p (h w) -> p h w", h=H) for v in range(WPI)]

        beaten = [bank[5 - b][0:T, 0:NT] for b in range(2)]

        dst_in, ew_in, src_rel_in = sem("dst_in"), sem("ew_in"), sem("src_rel_in")
        x_in, gru_in, pool_in, wrel_in, small_in = (sem(n) for n in (
            "x_in", "gru_in", "pool_in", "wrel_in", "small_in"))
        table1_out, scores_out, scores_in = sem("table1_out"), sem("scores_out"), sem("scores_in")
        table2_out = [sem("table2_out0"), sem("table2_out1")]
        result_out = sem("result_out")
        gathered = [[sem(f"gathered{L}_{v}") for v in range(WPI)] for L in range(2)]
        d_step, a_step, p_step = sem("dve_step"), sem("act_step"), sem("pool_step")
        gate_a, gate_p, gate_d, gate_pe = sem("gate_act"), sem("gate_pool"), sem("gate_dve"), sem("gate_pe")
        consts, columns_ready = sem("consts"), sem("columns_ready")
        edges_ready, pads_ready = sem("edges_ready"), sem("pads_ready")
        edges_turned, turned_kept = sem("edges_turned"), sem("turned_kept")
        gru_turned = sem("gru_turned")
        ln_var, ln_std, ln_ready, h_ready = (sem(n) for n in ("ln_var", "ln_std", "ln_ready", "h_ready"))
        chunk_ready, chunk_summed, deg_step = sem("chunk_ready"), sem("chunk_summed"), sem("deg_step")
        degw_ready, degw_turned, spread_ready, placed = (sem(n) for n in (
            "degw_ready", "degw_turned", "spread_ready", "placed"))
        deg_ready, deg_root, dinv_ready = sem("deg_ready"), sem("deg_root"), sem("dinv_ready")
        hp_ready, hp_ready_d, hp_turned, acc_init = (sem(n) for n in ("hp_ready", "hp_ready_d", "hp_turned", "acc_init"))
        psq_ready, pnorm_ready = sem("psq_ready"), sem("pnorm_ready")
        score_ready, score_turned, score_kept, tanh_ready = (sem(n) for n in (
            "score_ready", "score_turned", "score_kept", "tanh_ready"))
        rank_hot, rank_used, xt_kept = (sem(n) for n in ("rank_hot", "rank_used", "xt_kept"))
        gh_ready, gh_kept, rz_in = sem("gh_ready"), sem("gh_kept"), sem("rz_in")
        gates_ready, rz_ready, cand_in, cand_ready, w_ready = (sem(n) for n in (
            "gates_ready", "rz_ready", "cand_in", "cand_ready", "w_ready"))
        passes_ready = sem("passes_ready")
        idx_ready = [sem(f"idx_ready{L}") for L in range(2)]
        hot_step, hot_abs, hot_ready_a = sem("hot_step"), sem("hot_abs"), sem("hot_ready_act")
        rel_turned = sem("rel_turned")
        hot_ready = [sem(f"hot_ready{L}") for L in range(2)]
        win_summed = [sem(f"win_summed{L}") for L in range(2)]
        win_added = [sem(f"win_added{L}") for L in range(2)]
        pass_step = [sem(f"pass_step{L}") for L in range(2)]
        agg_done = [sem(f"agg_done{L}") for L in range(2)]
        tile_in, tile_mul, t_var, t_std, t_ln, h2_ready = (sem(n) for n in (
            "tile_in", "tile_mul", "t_var", "t_std", "t_ln", "h2_ready"))
        rows_free = [sem("rows_free0"), sem("rows_free1")]
        mask_ready, mask_used, counts_added, deg_summed = (sem(n) for n in (
            "mask_ready", "mask_used", "counts_added", "deg_summed"))
        h2_turned, h2_kept, prod_ready, prod_kept_a, prod_kept_d = (sem(n) for n in (
            "h2_turned", "h2_kept", "prod_ready", "prod_kept_a", "prod_kept_d"))
        t_step, cleared = sem("tile_step"), sem("cleared")
        bn_step, bn_var, bn_std, bn_ready = sem("bn_step"), sem("bn_var"), sem("bn_std"), sem("bn_ready")
        fin_in, fin_turned, fin_ready = sem("fin_in"), sem("fin_turned"), sem("fin_ready")

        block = ctx.enter_context(nc.Block())

        def loader(eng, name, n, low, high):
            regs = [eng.alloc_register(f"{name}{q}") for q in range(n)]

            def load(row):
                eng.load(regs, row)
                return [eng.snap(r, min_val=low, max_val=high) for r in regs]
            return load

        @block.sync
        def _(sp):
            for a, b, arrived in ((dst, dst_i, dst_in), (ew, ew_g, ew_in), (src, src_i, src_rel_in),
                                  (rel, rel_i, src_rel_in)):
                sp.dma_start(b[0:FULL, :], a[0:FULL * EW].rearrange("(g e) -> g e", e=EW)).then_inc(arrived, 16)
                sp.dma_start(b[FULL:NG, 0:LAST],
                             a[FULL * EW:E].rearrange("(g e) -> g e", g=1)).then_inc(arrived, 16)
                sp.dma_start(b[FULL:NG, LAST:EW],
                             a[E - EW + LAST:E].rearrange("(g e) -> g e", g=1)).then_inc(arrived, 16)
            for lo, hi in SPLIT:
                sp.dma_start(x_sb[lo:hi, :, :],
                             x.rearrange("(t p) f -> p t f", p=T)[lo:hi, :, :]).then_inc(x_in, 16)
            sp.dma_start(pbc[:, :], pool_p.rearrange("(a n) -> a n", a=1).broadcast_to([P, F])).then_inc(pool_in, 16)
            sp.dma_start(gru_raw[:, 0:6, :], wih.rearrange("(a p) f -> p a f", p=P)).then_inc(gru_in, 16)
            sp.dma_start(gru_raw[:, 6:12, :], whh.rearrange("(a p) f -> p a f", p=P)).then_inc(gru_in, 16)
            sp.dma_start(h0[:, :, :], w0.rearrange("(a p) f -> p a f", p=P)).then_inc(gru_in, 16)
            sp.dma_start(brow[:, 0, :], bih.rearrange("(a n) -> a n", a=1)).then_inc(small_in, 16)
            sp.dma_start(brow[:, 1, :], bhh.rearrange("(a n) -> a n", a=1)).then_inc(small_in, 16)
            for q, a in enumerate((gamma, beta)):
                for h in range(H):
                    sp.dma_start(gb[:, q, h:h + 1],
                                 a[P * h:P * (h + 1)].rearrange("(p a) -> p a", a=1)).then_inc(small_in, 16)
            for i in range(5):
                sp.wait_ge(hp_ready, i + 1)
                sp.wait_ge(hp_ready_d, 4 * (i + 1))
                for lo, hi in SPLIT:
                    sp.dma_start(table1.rearrange("(t p) f -> p t f", p=T)[lo:hi, 5 * i:5 * i + 5, :],
                                 hp[lo:hi, 5 * i:5 * i + 5, :]).then_inc(table1_out, 16)
            sp.wait_ge(score_kept, 1)
            sp.dma_start(score_row[:, :], score_t[:, :]).then_inc(scores_out, 16)
            sp.wait_ge(scores_out, 16)
            for lo, hi in SPLIT:
                sp.dma_start(s_all[lo:hi, :], score_row.rearrange("(a t) p -> a (t p)", a=1)
                             .broadcast_to([hi - lo, N])).then_inc(scores_in, 16)
            sp.wait_ge(table1_out, 16 * 10)
            sp.wait_ge(hp_turned, NT)
            sp.wait_ge(win_summed[0], 1)
            for k in range(H):
                sp.dma_start(wr[:, k, :].rearrange("p (r o) -> p r o", r=NREL),
                             wrel[:, P * k:P * (k + 1), :].rearrange("r p o -> p r o")).then_inc(wrel_in, 16)
            for q in range(2):
                sp.sem_inc(rows_free[q], 2)
            with sp.Fori(0, NT) as t:
                for q in range(2):
                    sp.wait_ge(prod_kept_a, t * 2 + (q + 4))
                    sp.wait_ge(prod_kept_d, t * 2 + (q + 4))
                    for lo, hi in SPLIT:
                        sp.dma_start(table2[ds(t * T + lo, hi - lo), 1024 * q:1024 * (q + 1)],
                                     rows2[lo:hi, 2 * q:2 * q + 2, :].rearrange("p c n -> p (c n)")
                                     ).then_inc(table2_out[q], 16)
                for q in range(2):
                    sp.wait_ge(table2_out[q], t * 32 + 32)
                    sp.sem_inc(rows_free[q], 1)
            for a, b in zip(CUTS, CUTS[1:]):
                sp.wait_ge(fin_ready, (b + 1) // 2)
                for lo, hi in SPLIT:
                    sp.dma_start(out.rearrange("(t p) f -> p t f", p=T)[lo:hi, a:b, :],
                                 x_sb[lo:hi, a:b, :]).then_inc(result_out, 16)
            sp.wait_ge(result_out, 16 * 2 * (len(CUTS) - 1))

        @block.gpsimd
        def _(pool):
            n = [0]

            def step(ins):
                n[0] += 1
                ins.then_inc(p_step, 1)
                pool.wait_ge(p_step, n[0])

            step(pool.iota(iota_i[:, :], [[1, IOTA]], base=0, channel_multiplier=0))
            pool.tensor_copy(iota[:, :], iota_i[:, :]).then_inc(consts, 1)
            step(pool.memset(ident[:, :], 0.0))
            pool.affine_select(out=ident[:, :], in_=ident[:, :], compare_op=ALU.not_equal, fill=1.0, base=0,
                               pattern=[[-1, P]], channel_multiplier=1).then_inc(consts, 1)
            pool.memset(ones[:, :], 1.0).then_inc(consts, 1)
            pool.memset(zrow[:, :], 0.0).then_inc(consts, 1)
            pool.wait_ge(edges_ready, 1)
            pool.affine_select(out=rel_g, in_=rel_g, compare_op=ALU.is_ge, fill=-10000.0, base=E - 1,
                               pattern=[[-1, EW]], channel_multiplier=-EW).then_inc(pads_ready, 1)
            pool.wait_ge(ew_in, 48)
            pool.affine_select(out=ew_g, in_=ew_g, compare_op=ALU.is_ge, fill=0.0, base=E - 1,
                               pattern=[[-1, EW]], channel_multiplier=-EW).then_inc(pads_ready, 1)
            step(pool.memset(lower[:, :], 1.0))
            pool.affine_select(out=lower[:, :], in_=lower[:, :], compare_op=ALU.is_gt, fill=0.0, base=0,
                               pattern=[[-1, T]], channel_multiplier=1).then_inc(consts, 1)
            pool.memset(ones_b[:, :], 1.0).then_inc(consts, 1)
            pool.memset(acc[:, :, N:APAD], 0.0).then_inc(consts, 1)

            def gather_rows(L, table):
                n_pass = pool.value_load(passes[0:1, 0:1], min_val=1, max_val=NPASS)
                with pool.Fori(0, n_pass) as w:
                    with pool.Fori(0, NIT) as i:
                        for v in range(WPI):
                            pool.wait_ge(idx_ready[L], (w * NIT + i) * WPI + (v + 1))
                            pool.sem_inc(gate_p, 1)
                            for k in range(BPW):
                                pool.indirect_dma_start(
                                    ring[:, BPW * v + k, :], None, table,
                                    bass.IndirectOffsetOnAxis(ap=idx_now[:, v, k:k + 1], axis=0),
                                ).then_inc(gathered[L][v], 16)

            pool.wait_ge(passes_ready, 1)
            pool.wait_ge(table1_out, 16 * 10)
            gather_rows(0, table1[:, :])
            pool.wait_ge(tile_in, NT)
            pool.memset(acc[:, :, :], 0.0).then_inc(cleared, 1)
            for q in range(2):
                pool.wait_ge(table2_out[q], 2 * 16 * NT)
            gather_rows(1, table2_rows)

        @block.scalar
        def _(act):
            def stage_first(L, table):
                for v in range(WPI):
                    act.activation(idx_now[:, v, :], table[:, :, v], ACT.Copy).then_inc(idx_ready[L], 1)

            act.wait_ge(consts, 1)
            act.activation(iota_rep, iota[:, 0:W].unsqueeze(2).broadcast_to([P, W, NG]), ACT.Copy).then_inc(columns_ready, 1)
            for n, (b, to) in enumerate(((2, rel_t[:, :, 0:NG]), (3, ew_t[:, :, 0:NG]),
                                         (4, src_t[:, :, 0:NG]), (5, idx2_t[:, :, 0:NG]))):
                act.wait_ge(edges_turned, n + 1)
                act.activation(to, bank[b][:, 0:BPW * NG].rearrange("p (k g) -> p k g", k=BPW),
                               ACT.Copy).then_inc(turned_kept, 1)
            act.wait_ge(turned_kept, 4)
            for a in (src_t, idx2_t, rel_t, ew_t):
                act.activation(a[:, :, NG:NG + WPI], a[:, :, 0:WPI], ACT.Copy).then_inc(a_step, 1)
            act.wait_ge(a_step, 4)
            stage_first(0, src_t)
            for n in range(8):
                k, g = n // 4, n % 4
                c0, c1 = 512 * g, min(512 * (g + 1), 14 * P)
                act.wait_ge(gru_turned, n + 1)
                act.activation(gru_t[:, k, c0:c1], bank[2 + n % 4][:, 0:c1 - c0], ACT.Copy).then_inc(turned_kept, 1)
            act.wait_ge(ln_var, 1)
            act.activation(rstd[0:T, :], rstd[0:T, :], ACT.Sqrt).then_inc(ln_std, 1)
            act.wait_ge(psq_ready, 1)
            act.activation(psq[:, 1:2], psq[:, 0:1], ACT.Sqrt).then_inc(pnorm_ready, 1)
            act.wait_ge(deg_ready, 1)
            act.activation(dtmp[0:T, 2, :], dtmp[0:T, 1, :], ACT.Sqrt).then_inc(deg_root, 1)
            for t in range(NT):
                act.activation(h_sb[0:T, t, :], x_sb[0:T, t, :], ACT.Relu, bias=nbias[0:T, t:t + 1],
                               scale=rstd[0:T, t:t + 1]).then_inc(h_ready, 1)
                if t % 5 == 4:
                    act.wait_ge(dinv_ready, 1)
                    act.wait_ge(h_ready, t + 1)
                    act.activation(hp[0:T, t, :], h_sb[0:T, t, :], ACT.Copy,
                                   scale=dinv[0:T, t:t + 1]).then_inc(hp_ready, 1)
            act.wait_ge(score_ready, 1)
            act.activation(th[0:T, :], score[0:T, 1, :], ACT.Tanh).then_inc(tanh_ready, 1)
            for t in range(NT):
                act.wait_ge(hp_turned, t + 1)
                act.activation(acc[:, :, T * t:T * (t + 1)],
                               bank[t % 4][:, 0:H * T].rearrange("p (h n) -> p h n", h=H),
                               ACT.Copy).then_inc(acc_init, 1)
            def stage(L, table, w, i, v):
                act.wait_ge(win_summed[L], (w * NIT + i) * WPI + (v + 1))
                act.sem_inc(gate_a, 1)
                act.activation(idx_now[:, v, :],
                               table[:, :, ds(i * WPI + (WPI + v), 1)].rearrange("p k a -> p (k a)"),
                               ACT.Copy).then_inc(idx_ready[L], 1)

            def stage_next(L, table, w, i):
                for v in range(WPI):
                    stage(L, table, w, i, v)

            def stage_more(L, table, n_pass):
                with act.If(n_pass > 1):
                    with act.Fori(1, n_pass) as w:
                        with act.Fori(0, NIT) as i:
                            stage_next(L, table, w, i)
                act.sem_inc(gate_a, 1)

            def take_tile(t):
                act.wait_ge(cand_ready, 2)
                act.wait_ge(w_ready, 2)
                act.wait_ge(tile_mul, t + 1)
                act.sem_inc(gate_a, 1)
                act.activation(s_tile[:, :, :], acc[:, :, ds(t * T, T)], ACT.Copy).then_inc(tile_in, 1)

            def norm_root(t):
                act.wait_ge(t_var, t + 1)
                act.sem_inc(gate_a, 1)
                act.activation(ln[0:T, 9:10], ln[0:T, 8:9], ACT.Sqrt).then_inc(t_std, 1)

            def norm_relu(t):
                act.wait_ge(t_ln, t + 1)
                act.wait_ge(h2_turned, t + 1)
                act.sem_inc(gate_a, 1)
                act.activation(h2[0:T, :], x_sb[0:T, ds(t, 1), :].rearrange("p a f -> p (a f)"), ACT.Relu,
                               bias=ln[0:T, 11:12], scale=ln[0:T, 10:11]).then_inc(h2_ready, 1)

            def keep_h2(t):
                act.wait_ge(h2_turned, t + 2)
                act.sem_inc(gate_a, 1)
                act.activation(h2_t[:, :, :], bank[5][:, 0:H * T].rearrange("p (h n) -> p h n", h=H),
                               ACT.Copy).then_inc(h2_kept, 1)

            def keep_rows(t, q):
                act.wait_ge(prod_ready, t * 4 + (2 * q + 5))
                act.wait_ge(rows_free[q], t + 2)
                act.sem_inc(gate_a, 1)
                act.activation(rows2[0:T, 2 * q, :], bank[6][0:T, :], ACT.Copy).then_inc(prod_kept_a, 1)

            act.sem_inc(h2_ready, 1)
            act.sem_inc(h2_kept, 1)
            act.sem_inc(prod_kept_a, 3)
            act.wait_ge(passes_ready, 1)
            n_pass = act.value_load(passes[0:1, 0:1], min_val=1, max_val=NPASS)
            def hot(i, v):
                g, at = i * WPI + v, (i - 1) * WPI + v
                for k in range(BPW):
                    last = act.activation(hot_tmp[:, 0, k, :], iota_w0[:, :], ACT.Abs, bias=rel_neg[:, k, g:g + 1])
                last.then_inc(hot_abs, 1)
                act.wait_ge(hot_abs, 2 * at + 1)
                act.activation(hot_tmp[:, 1, :, :], hot_tmp[:, 0, :, :], ACT.Relu, bias=1.0, scale=-1.0).then_inc(hot_abs, 1)
                act.wait_ge(hot_abs, 2 * at + 2)
                for k in range(BPW):
                    last = act.activation(onehot[:, v, k, :], hot_tmp[:, 1, k, :], ACT.Copy, scale=ew_t[:, k, g:g + 1])
                last.then_inc(hot_ready_a, 1)

            act.wait_ge(rel_turned, 1)
            for i in range(GRU_IT):
                for v in range(WPI):
                    stage(0, src_t, 0, i, v)
                    hot(i + 1, v)
            stage(0, src_t, 0, GRU_IT, 0)
            stage(0, src_t, 0, GRU_IT, 1)
            for m in range(H):
                act.wait_ge(rz_in, m + 1)
                act.activation(rz[:, m, :], rz[:, m, :], ACT.Sigmoid).then_inc(rz_ready, 1)
                stage(0, src_t, 0, GRU_IT, 2 + m)
            for m in range(H):
                act.wait_ge(cand_in, m + 1)
                act.activation(cand[:, m, :], gtmp[:, m, :], ACT.Tanh).then_inc(cand_ready, 1)
            load_flags, load_two = loader(act, "flag", GT + 1, 0, 1), loader(act, "two", 2, 0, 1)
            t0 = act.value_load(passes[0:1, 1:2], min_val=0, max_val=EARLY)
            more = act.value_load(passes[0:1, 2:3], min_val=0, max_val=1)
            pending = act.value_load(taken_one[0:1, EARLY - GROUPS * GT - 1, 1:2], min_val=0, max_val=1)

            def turn(i0, first, end, t, take, took):
                for n, s in enumerate(range(first, end)):
                    i = i0 + s // WPI
                    stage(0, src_t, 0, i, s % WPI)
                    if n == 0:
                        with act.If(take > 0):
                            act.wait_ge(win_added[0], i * WPI)
                            act.sem_inc(gate_a, 1)
                            take_tile(t)
                        with act.If(took > 0):
                            keep_rows(t - 1, 0)
                    if n == 1:
                        with act.If(take > 0):
                            norm_root(t)
                            norm_relu(t)
                    if n == 2:
                        with act.If(took > 0):
                            keep_rows(t - 1, 1)
                with act.If(take > 0):
                    keep_h2(t)
                act.sem_inc(gate_a, 1)

            with act.Fori(0, GROUPS) as g:
                flags = load_flags(taken[0:1, ds(g, 1), 0:GT + 1].rearrange("p a q -> p (a q)"))
                for j, (first, end) in enumerate(TURNS):
                    turn(g * GIT + FIRST_IT, first, end, g * GT + j, flags[j + 1], flags[j])
            with act.Fori(SINGLE_IT, NIT) as i:
                took, take = load_two(taken_one[0:1, ds(i - SINGLE_IT, 1), 0:2].rearrange("p a q -> p (a q)"))
                turn(i, 0, WPI, i - LAG, take, took)
            stage_more(0, src_t, n_pass)
            with act.If(pending > 0):
                keep_rows(EARLY - 1, 0)
            act.wait_ge(agg_done[0], 1)
            act.sem_inc(gate_a, 1)
            take_tile(t0)
            norm_root(t0)
            norm_relu(t0)
            with act.If(pending > 0):
                keep_rows(EARLY - 1, 1)
            act.sem_inc(gate_a, 1)
            with act.If(more > 0):
                with act.Fori(t0, NT - 1) as t:
                    keep_h2(t)
                    take_tile(t + 1)
                    keep_rows(t, 0)
                    norm_root(t + 1)
                    norm_relu(t + 1)
                    keep_rows(t, 1)
            act.sem_inc(gate_a, 1)
            keep_h2(NT - 1)
            for q in range(2):
                keep_rows(NT - 1, q)

            stage_first(1, idx2_t)
            with act.Fori(0, NIT) as i:
                stage_next(1, idx2_t, 0, i)
            stage_more(1, idx2_t, n_pass)
            act.wait_ge(bn_var, 1)
            act.activation(bn[:, :, 3], bn[:, :, 2], ACT.Sqrt).then_inc(bn_std, 1)
            act.wait_ge(bn_ready, 1)
            for first, end in zip(CUTS, CUTS[1:]):
                for h in range(H):
                    a = acc[:, h, T * first:T * end]
                    last = act.activation(a, a, ACT.Identity, bias=bn[:, h, 6:7], scale=bn[:, h, 5:6])
                last.then_inc(fin_in, 1)

        @block.vector
        def _(dve):
            n = [0]

            def step(ins):
                n[0] += 1
                ins.then_inc(d_step, 1)
                dve.wait_ge(d_step, n[0])

            dve.wait_ge(dst_in, 48)
            step(dve.tensor_copy(dst_f, dst_i))
            step(dve.tensor_reduce(span[0:NG, 0:1], dst_f, AX.X, ALU.min))
            dve.tensor_scalar(rel_g, dst_f, span[0:NG, 0:1], None, ALU.subtract).then_inc(edges_ready, 1)
            step(dve.tensor_reduce(span[0:NG, 1:2], dst_f, AX.X, ALU.max))
            step(dve.tensor_tensor(span[0:NG, 2:3], span[0:NG, 1:2], span[0:NG, 0:1], ALU.subtract))
            dve.wait_ge(src_rel_in, 96)
            step(dve.tensor_copy(src_g, src_i))
            dve.scalar_tensor_tensor(idx2_g, src_i, float(NREL), rel_i, ALU.mult, ALU.add).then_inc(edges_ready, 1)

            dve.wait_ge(turned_kept, 2)
            ew_k = ew_t[:, :, 0:NG]
            by_k = [a.rearrange("p (k g) -> p k g", k=BPW) for a in (ewp[:, 0, :], ew_r[:, 0, :])]
            step(dve.tensor_copy(by_k[0], ew_k))
            step(dve.tensor_tensor(by_k[1], ew_k, by_k[0], ALU.subtract))
            step(dve.tensor_copy(ewp[:, 1, :], ew_r[:, 0, :]))
            step(dve.tensor_tensor(ew_r[:, 1, :], ew_r[:, 0, :], ewp[:, 1, :], ALU.subtract))
            step(dve.tensor_copy(ewp[:, 2, :], ew_r[:, 1, :]))

            step(dve.memset(shift[:, :], 0.0))
            step(dve.tensor_copy(shift[0:NG, 1:2], span[0:NG, 0:1]))
            step(dve.memset(deg[0:T, :], 1.0))

            def window_hots(p):
                d = [p * 16]

                def dstep(ins):
                    d[0] = d[0] + 1
                    ins.then_inc(deg_step, 1)
                    dve.wait_ge(deg_step, d[0])
                    dve.sem_inc(gate_d, 1)

                dstep(dve.tensor_scalar(rel_b[:, :, :], rel_t[:, :, 0:NG], shift[:, 0:1], None, ALU.subtract))
                for k in range(BPW):
                    dve.wait_ge(chunk_summed, p * BPW + (k + 1))
                    dve.sem_inc(gate_d, 1)
                    dve.tensor_tensor(oh_b[k % 2], iota_rep, rel_b[:, k, :].unsqueeze(1).broadcast_to([P, W, NG]),
                                      ALU.is_equal).then_inc(chunk_ready, 1)
                dstep(dve.tensor_scalar(where[0:NG, 0:1], shift[0:NG, 1:2], 1.0 / T, 0.5 / T - 0.5, ALU.mult, ALU.add))
                dstep(dve.tensor_scalar(where[0:NG, 1:2], where[0:NG, 0:1], MAGIC, MAGIC, ALU.add, ALU.subtract))
                dstep(dve.scalar_tensor_tensor(where[0:NG, 2:3], where[0:NG, 1:2], -float(T), shift[0:NG, 1:2],
                                               ALU.mult, ALU.add))
                dve.tensor_scalar(base_lo, iota[0:NG, :], float(W - 1), where[0:NG, 2:3],
                                  ALU.subtract, ALU.is_equal).then_inc(spread_ready, 1)
                dstep(dve.tensor_scalar(base_hi, iota[0:NG, 0:HC], 1.0, where[0:NG, 1:2], ALU.subtract, ALU.is_equal))

            def place_sums(p):
                d = [p * 16 + 5]

                def dstep(ins):
                    d[0] = d[0] + 1
                    ins.then_inc(deg_step, 1)
                    dve.wait_ge(deg_step, d[0])
                    dve.sem_inc(gate_d, 1)

                dve.wait_ge(deg_summed, p + 1)
                dve.sem_inc(gate_d, 1)
                dstep(dve.tensor_copy(degs, bank[0][0:W, 0:3 * NG]))
                dstep(dve.tensor_tensor(deg_w, degs[:, NG:2 * NG], degs[:, 2 * NG:3 * NG], ALU.add))
                dve.tensor_tensor(deg_w, deg_w, degs[:, 0:NG], ALU.add).then_inc(degw_ready, 1)
                dve.wait_ge(degw_turned, p + 1)
                dve.sem_inc(gate_d, 1)
                turned = bank[1][0:NG, 0:W]
                dstep(dve.tensor_copy(deg_p[:, 0, :], turned))
                dstep(dve.tensor_tensor(deg_g[:, 0, :], turned, deg_p[:, 0, :], ALU.subtract))
                dstep(dve.tensor_copy(deg_p[:, 1, :], deg_g[:, 0, :]))
                dstep(dve.tensor_tensor(deg_g[:, 1, :], deg_g[:, 0, :], deg_p[:, 1, :], ALU.subtract))
                dstep(dve.tensor_copy(deg_p[:, 2, :], deg_g[:, 1, :]))
                for q in range(3):
                    last = dve.tensor_tensor(spread[:, q, :, :], deg_p[:, q, :].unsqueeze(2).broadcast_to([NG, W, HC]),
                                             base_hi.unsqueeze(1).broadcast_to([NG, W, HC]), ALU.mult)
                last.then_inc(spread_ready, 1)

            def keep_degrees(p):
                dve.wait_ge(placed, p + 1)
                dve.sem_inc(gate_d, 1)
                for q in range(3):
                    at = p * 16 + (13 + q)
                    dve.tensor_tensor(deg[0:T, :], deg[0:T, :], bank[6][0:T, NT * q:NT * (q + 1)],
                                      ALU.add).then_inc(deg_step, 1)
                    dve.wait_ge(deg_step, at)
                    dve.sem_inc(gate_d, 1)

            def next_shift(p):
                dve.tensor_scalar(shift[:, :], shift[:, :], float(W), None, ALU.add).then_inc(deg_step, 1)
                dve.wait_ge(deg_step, p * 16)
                dve.sem_inc(gate_d, 1)

            dve.wait_ge(columns_ready, 1)
            window_hots(0)


            dve.wait_ge(edges_turned, 5)
            dve.wait_ge(consts, 7)
            dve.tensor_copy(base_row[:, 0, :], bank[6][0:1, 0:NG])
            step(dve.tensor_copy(base_row[:, 1, :], bank[6][0:1, 0:NG]))
            dve.tensor_copy(base_i[:, :], base_row[:, 0, :])
            step(dve.tensor_reduce(flag[:, 0:1], bank[6][0:1, P:P + NG], AX.X, ALU.max))
            step(dve.tensor_scalar(flag[:, 1:2], flag[:, 0:1], 1.0 / W, 0.5 / W - 0.5, ALU.mult, ALU.add))
            step(dve.tensor_scalar(flag[:, 1:2], flag[:, 1:2], MAGIC, MAGIC, ALU.add, ALU.subtract))
            dve.tensor_scalar(passes[:, 0:1], flag[:, 1:2], 1.0, None, ALU.add)
            step(dve.tensor_scalar(flag[:, 2:3], flag[:, 1:2], 0.5, None, ALU.is_lt))
            step(dve.memset(least[:, :, :], 1e9))
            step(dve.tensor_reduce(least[:, 0, 0:NIT], base_row[:, 0, :].rearrange("p (i v) -> p i v", v=WPI),
                                   AX.X, ALU.min))
            for q, d in enumerate((1, 2, 4, 8, 16)):
                step(dve.tensor_tensor(least[:, 1 - q % 2, 0:NIT], least[:, q % 2, 0:NIT], least[:, q % 2, d:NIT + d],
                                       ALU.min))
            for j, (first, _) in enumerate(TURNS):
                at = FIRST_IT + first // WPI
                dve.tensor_copy(early[:, 3, 0:GROUPS * GT].rearrange("p (g j) -> p g j", j=GT)[:, :, j],
                                least[:, 1, at:at + GROUPS * GIT].rearrange("p (g j) -> p g j", j=GIT)[:, :, 0])
            dve.tensor_copy(early[:, 3, GROUPS * GT:EARLY], least[:, 1, SINGLE_IT:NIT])
            step(dve.tensor_scalar(early[:, 0, :], iota[0:1, 0:EARLY], float(T), float(T), ALU.mult, ALU.add))
            step(dve.tensor_tensor(early[:, 1, :], early[:, 3, :], early[:, 0, :], ALU.is_ge))
            step(dve.tensor_tensor_scan(early[:, 2, :], early[:, 1, :], zrow[0:1, 0:EARLY], flag[:, 2:3],
                                        ALU.mult, ALU.add))
            step(dve.tensor_reduce(flag[:, 3:4], early[:, 2, :], AX.X, ALU.add))
            dve.memset(taken[:, 0, 0:1], 0)
            dve.tensor_copy(taken[:, :, 1:GT + 1], early[:, 2, 0:GROUPS * GT].rearrange("p (g j) -> p g j", j=GT))
            dve.tensor_copy(taken[:, 1:GROUPS, 0:1], early[:, 2, GT - 1:(GROUPS - 1) * GT + GT - 1].rearrange(
                "p (g j) -> p g j", j=GT)[:, :, 0:1])
            dve.tensor_copy(taken_one[:, :, 0], early[:, 2, GROUPS * GT - 1:EARLY - 1])
            dve.tensor_copy(taken_one[:, :, 1], early[:, 2, GROUPS * GT:EARLY])
            dve.tensor_copy(passes[:, 1:2], flag[:, 3:4])
            step(dve.tensor_scalar(passes[:, 2:3], flag[:, 3:4], float(NT - 1), None, ALU.is_lt))
            dve.sem_inc(passes_ready, 1)
            place_sums(0)

            dve.wait_ge(x_in, 32)
            for t in range(NT):
                last = dve.bn_stats(st6[0:T, t, :], x_sb[0:T, t, :])
            step(last)
            for t in range(NT):
                last = dve.bn_aggr(mv[0:T, t, :], st6[0:T, t, :])
            step(last)
            dve.tensor_scalar(rstd[0:T, :], mv[0:T, :, 1], EPS, None, ALU.add).then_inc(ln_var, 1)
            dve.wait_ge(pool_in, 16)
            dve.tensor_tensor_reduce(out=oh_rank[:, 0, :], in0=pbc[:, :], in1=pbc[:, :], scale=1.0, scalar=0.0,
                                     op0=ALU.mult, op1=ALU.add, accum_out=psq[:, 0:1]).then_inc(psq_ready, 1)
            dve.wait_ge(ln_std, 1)
            step(dve.reciprocal(rstd[0:T, :], rstd[0:T, :]))
            dve.scalar_tensor_tensor(nbias[0:T, :], mv[0:T, :, 0], -1.0, rstd[0:T, :], ALU.mult,
                                     ALU.mult).then_inc(ln_ready, 1)

            keep_degrees(0)
            n_pass = dve.value_load(passes[0:1, 0:1], min_val=1, max_val=NPASS)
            with dve.If(n_pass > 1):
                with dve.Fori(1, n_pass) as p:
                    next_shift(p)
                    window_hots(p)
                    place_sums(p)
                    keep_degrees(p)
            dve.sem_inc(gate_d, 1)
            step(dve.tensor_scalar(dtmp[0:T, 3, :], deg[0:T, :], 0.0, None, ALU.is_gt))
            dve.tensor_scalar(dtmp[0:T, 1, :], deg[0:T, :], 1e-30, None, ALU.max).then_inc(deg_ready, 1)
            dve.wait_ge(deg_root, 1)
            step(dve.reciprocal(dinv[0:T, :], dtmp[0:T, 2, :]))
            dve.tensor_tensor(dinv[0:T, :], dinv[0:T, :], dtmp[0:T, 3, :], ALU.mult).then_inc(dinv_ready, 1)

            base = n[0]
            for t in range(NT):
                dve.wait_ge(h_ready, t + 1)
                if t >= 3:
                    dve.wait_ge(d_step, base + t - 2)
                dve.tensor_tensor_reduce(out=oh_rank[0:T, 1 + t % 3, :], in0=h_sb[0:T, t, :], in1=pbc[0:T, :],
                                         scale=1.0, scalar=0.0, op0=ALU.mult, op1=ALU.add,
                                         accum_out=score[0:T, 0, t:t + 1]).then_inc(d_step, 1)
                if t == 0:
                    dve.wait_ge(dinv_ready, 1)
                if t % 5 < 4:
                    dve.tensor_scalar(hp[0:T, t, :], h_sb[0:T, t, :], dinv[0:T, t:t + 1], None,
                                      ALU.mult).then_inc(hp_ready_d, 1)
            n[0] += NT
            dve.wait_ge(d_step, n[0])
            dve.wait_ge(pnorm_ready, 1)
            step(dve.reciprocal(psq[:, 2:3], psq[:, 1:2]))
            dve.tensor_scalar(score[0:T, 1, :], score[0:T, 0, :], psq[0:T, 2:3], None, ALU.mult).then_inc(score_ready, 1)
            dve.wait_ge(score_turned, 1)
            dve.tensor_copy(score_t[:, :], bank[6][0:NT, 0:T]).then_inc(score_kept, 1)
            dve.wait_ge(gh_ready, 1)
            for m in range(H):
                dve.tensor_copy(gh[:, m, 0:2 * F], bank[4 + m][:, :])
                last = dve.tensor_copy(gh[:, m, 2 * F:3 * F], bank[7][:, F * m:F * (m + 1)])
            last.then_inc(gh_kept, 1)
            step(dve.memset(outdone[0:T, :], 0.0))

            def hot(L, w, i, v):
                g = i * WPI + v
                last = dve.tensor_tensor(onehot[:, v, :, :], iota_w[:, :].unsqueeze(1).broadcast_to([P, BPW, W]),
                                         rel_t[:, :, ds(g, 1)].broadcast_to([P, BPW, W]), ALU.is_equal)
                if L == 0:
                    last.then_inc(hot_step, 1)
                    dve.wait_ge(hot_step, (w * (NIT + 1) + i) * WPI + (v + 1))
                    dve.sem_inc(gate_d, 1)
                    last = dve.tensor_tensor(onehot[:, v, :, :], onehot[:, v, :, :],
                                             ew_t[:, :, ds(g, 1)].broadcast_to([P, BPW, W]), ALU.mult)
                last.then_inc(hot_ready[L], 1)

            def first_hots(L, w):
                for v in range(WPI):
                    hot(L, w, 0, v)

            base_loader = loader(dve, "base", WPI, 0, N)

            def load_bases(i):
                return base_loader(base_i[0:1, ds(i * WPI, WPI)])

            def add_sums(L, w, i, v, base):
                at = acc[:, :, ds(base[v], W)]
                dve.wait_ge(win_summed[L], (w * NIT + i) * WPI + (v + 1))
                dve.tensor_tensor(at, at, win[v], ALU.add).then_inc(win_added[L], 1)
                dve.wait_ge(win_added[L], (w * NIT + i) * WPI + (v + 1))

            def add_hot(L, w, i, v, base):
                add_sums(L, w, i, v, base)
                hot(L, w, i + 1, v)

            def add_hots(L, w, i):
                base = load_bases(i)
                for v in range(WPI):
                    add_hot(L, w, i, v, base)

            def more_passes(L, n_pass):
                dve.wait_ge(hot_ready[L], (NIT + 1) * WPI)
                with dve.If(n_pass > 1):
                    with dve.Fori(1, n_pass) as w:
                        dve.tensor_scalar(iota_w[:, :], iota_w[:, :], float(W), None, ALU.add).then_inc(pass_step[L], 1)
                        dve.tensor_scalar(base_row[:, 1, :], base_row[:, 1, :], float(W), float(N), ALU.add,
                                          ALU.min).then_inc(pass_step[L], 1)
                        dve.wait_ge(pass_step[L], w * 3 - 1)
                        dve.sem_inc(gate_d, 1)
                        dve.tensor_copy(base_i[:, :], base_row[:, 1, :]).then_inc(pass_step[L], 1)
                        dve.wait_ge(pass_step[L], w * 3)
                        dve.sem_inc(gate_d, 1)
                        first_hots(L, w)
                        with dve.Fori(0, NIT) as i:
                            add_hots(L, w, i)
                        dve.wait_ge(hot_ready[L], (w + 1) * ((NIT + 1) * WPI))
                        dve.sem_inc(gate_d, 1)
                dve.sem_inc(gate_d, 1)

            def compare_tile(t):
                if t >= 2:
                    dve.wait_ge(mask_used, t - 1)
                own = score[0:T, 1, t:t + 1]
                dve.tensor_scalar(mask[t % 2][0:T, 0:N - T * t], s_all[:, T * t:N], own, 0.0,
                                  ALU.is_gt, ALU.add, accum_out=cnt[0:T, t, 0:1]).then_inc(mask_ready, 1)
                step(dve.scalar_tensor_tensor(cmp_out[0:T, t % 2, :], s_all[:, T * t:T * (t + 1)], own, lower[0:T, :],
                                              ALU.is_equal, ALU.mult, accum_out=cnt[0:T, t, 1:2]))

            def add_counts(t):
                dve.wait_ge(mask_used, t + 1)
                dve.tensor_tensor(outdone[0:T, t + 1:NT], outdone[0:T, t + 1:NT], beaten[t % 2][:, t + 1:NT],
                                  ALU.add).then_inc(counts_added, 1)
                dve.wait_ge(counts_added, t + 1)

            def rank_tiles(a, b):
                dve.wait_ge(mask_ready, b)
                step(dve.tensor_tensor(rtmp[0:T, 0, a:b], cnt[0:T, a:b, 0], cnt[0:T, a:b, 1], ALU.add))
                step(dve.tensor_tensor(rtmp[0:T, 1, a:b], rtmp[0:T, 0, a:b], outdone[0:T, a:b], ALU.subtract))
                step(dve.scalar_tensor_tensor(rank[0:T, a:b], iota[0:T, a:b], float(T), rtmp[0:T, 1, a:b],
                                              ALU.mult, ALU.add))

            def hot_rank(t):
                if t >= 4:
                    dve.wait_ge(rank_used, t - 3)
                dve.tensor_scalar(oh_rank[0:T, t % 4, :], iota[0:T, 0:F], rank[0:T, t:t + 1], th[0:T, t:t + 1],
                                  ALU.is_equal, ALU.mult).then_inc(rank_hot, 1)

            step(dve.tensor_copy(iota_w[:, :], iota[:, 0:W]))
            dve.tensor_copy(iota_w0[:, :], iota[:, 0:W])
            step(dve.tensor_scalar(rel_neg[:, :, :], rel_t[:, :, 0:FIRST_IT * WPI], -1.0, None, ALU.mult))
            dve.sem_inc(rel_turned, 1)
            first_hots(0, 0)
            dve.wait_ge(scores_in, 32)
            for t in COMPARED_FIRST:
                compare_tile(t)
            dve.wait_ge(acc_init, NT)
            dve.wait_ge(tanh_ready, 1)
            before = COMPARED_FIRST
            for i in range(GRU_IT):
                base = load_bases(i)
                for v in range(WPI):
                    add_sums(0, 0, i, v, base)
                    at = i * WPI + v
                    tiles = COMPARED[at] if at < len(COMPARED) else []
                    if tiles:
                        compare_tile(tiles[0])
                    for t in before:
                        if t < NT - 1:
                            add_counts(t)
                    for t in tiles[1:]:
                        compare_tile(t)
                    before = tiles
                    if at in RANKED:
                        rank_tiles(*RANKED[at])
                    for t in HOT_RANKS.get(at, []):
                        hot_rank(t)
            dve.wait_ge(rank_used, NT)
            dve.tensor_copy(xt[:, 0, :], bank[6][:, 0:F]).then_inc(xt_kept, 1)
            dve.tensor_copy(xt[:, 1, :], bank[7][:, 0:F]).then_inc(xt_kept, 1)
            dve.sem_inc(hot_step, GRU_IT * WPI)
            dve.sem_inc(hot_ready[0], GRU_IT * WPI)
            base = load_bases(GRU_IT)
            dve.wait_ge(gh_kept, 1)
            add_hot(0, 0, GRU_IT, 0, base)
            add_hot(0, 0, GRU_IT, 1, base)
            for m in range(H):
                dve.wait_ge(gates_ready, 2 * m + 1)
                dve.tensor_tensor(rz[:, m, :], bank[4 + m][:, :], gh[:, m, 0:2 * F], ALU.add).then_inc(rz_in, 1)
                add_hot(0, 0, GRU_IT, 2 + m, base)
            for m in range(H):
                dve.wait_ge(rz_ready, m + 1)
                dve.wait_ge(gates_ready, 2 * m + 2)
                step(dve.tensor_tensor(gtmp[:, m, :], rz[:, m, 0:F], gh[:, m, 2 * F:3 * F], ALU.mult))
                dve.tensor_tensor(gtmp[:, m, :], gtmp[:, m, :], bank[6 + m][:, 0:F], ALU.add).then_inc(cand_in, 1)
            for m in range(H):
                dve.wait_ge(cand_ready, m + 1)
                step(dve.tensor_tensor(w_new[:, m, :], h0[:, m, :], cand[:, m, :], ALU.subtract))
                step(dve.tensor_tensor(w_new[:, m, :], w_new[:, m, :], rz[:, m, F:2 * F], ALU.mult))
                dve.tensor_tensor(w_new[:, m, :], w_new[:, m, :], cand[:, m, :], ALU.add).then_inc(w_ready, 1)

            def norm_stats(t):
                row = x_sb[0:T, ds(t, 1), :].rearrange("p a f -> p (a f)")
                dve.wait_ge(h2_ready, t + 1)
                dve.wait_ge(tile_mul, t + 2)
                dve.scalar_tensor_tensor(row, bank[4][0:T, 0:F], dinv[0:T, ds(t, 1)], row, ALU.mult,
                                         ALU.add).then_inc(t_step, 1)
                dve.wait_ge(t_step, t * 4 + 1)
                dve.sem_inc(gate_d, 1)
                dve.bn_stats(ln[0:T, 0:6], row).then_inc(t_step, 1)
                dve.wait_ge(t_step, t * 4 + 2)
                dve.sem_inc(gate_d, 1)
                dve.bn_aggr(ln[0:T, 6:8], ln[0:T, 0:6]).then_inc(t_step, 1)
                dve.wait_ge(t_step, t * 4 + 3)
                dve.tensor_scalar(ln[0:T, 8:9], ln[0:T, 7:8], EPS, None, ALU.add).then_inc(t_var, 1)

            def norm_scale(t):
                dve.wait_ge(t_std, t + 1)
                dve.reciprocal(ln[0:T, 10:11], ln[0:T, 9:10]).then_inc(t_step, 1)
                dve.wait_ge(t_step, t * 4 + 4)
                dve.tensor_scalar(ln[0:T, 11:12], ln[0:T, 6:7], ln[0:T, 10:11], -1.0, ALU.mult, ALU.mult).then_inc(t_ln, 1)

            def keep_rows(t, q):
                dve.wait_ge(prod_ready, t * 4 + (2 * q + 6))
                dve.wait_ge(rows_free[q], t + 2)
                dve.sem_inc(gate_d, 1)
                dve.tensor_copy(rows2[0:T, 2 * q + 1, :], bank[7][0:T, :]).then_inc(prod_kept_d, 1)

            dve.sem_inc(prod_kept_d, 3)
            load_flags, load_two = loader(dve, "flag", GT + 1, 0, 1), loader(dve, "two", 2, 0, 1)
            t0 = dve.value_load(passes[0:1, 1:2], min_val=0, max_val=EARLY)
            more = dve.value_load(passes[0:1, 2:3], min_val=0, max_val=1)
            pending = dve.value_load(taken_one[0:1, EARLY - GROUPS * GT - 1, 1:2], min_val=0, max_val=1)

            def turn(i0, first, end, t, take, took, base):
                for n, s in enumerate(range(first, end)):
                    i = i0 + s // WPI
                    if s % WPI == 0:
                        base[:] = load_bases(i)
                    add_hot(0, 0, i, s % WPI, base)
                    if n == 1:
                        with dve.If(take > 0):
                            norm_stats(t)
                        with dve.If(took > 0):
                            keep_rows(t - 1, 0)
                        with dve.If(take > 0):
                            norm_scale(t)
                with dve.If(took > 0):
                    keep_rows(t - 1, 1)
                dve.sem_inc(gate_d, 1)

            with dve.Fori(0, GROUPS) as g:
                base = []
                flags = load_flags(taken[0:1, ds(g, 1), 0:GT + 1].rearrange("p a q -> p (a q)"))
                for j, (first, end) in enumerate(TURNS):
                    turn(g * GIT + FIRST_IT, first, end, g * GT + j, flags[j + 1], flags[j], base)
            with dve.Fori(SINGLE_IT, NIT) as i:
                took, take = load_two(taken_one[0:1, ds(i - SINGLE_IT, 1), 0:2].rearrange("p a q -> p (a q)"))
                turn(i, 0, WPI, i - LAG, take, took, [])
            more_passes(0, n_pass)
            dve.sem_inc(agg_done[0], 1)
            with dve.If(pending > 0):
                keep_rows(EARLY - 1, 0)
            norm_stats(t0)
            norm_scale(t0)
            with dve.If(pending > 0):
                keep_rows(EARLY - 1, 1)
            dve.sem_inc(gate_d, 1)
            with dve.If(more > 0):
                with dve.Fori(t0, NT - 1) as t:
                    norm_stats(t + 1)
                    keep_rows(t, 0)
                    norm_scale(t + 1)
                    keep_rows(t, 1)
            dve.sem_inc(gate_d, 1)
            for q in range(2):
                keep_rows(NT - 1, q)

            dve.wait_ge(cleared, 1)
            step(dve.tensor_copy(iota_w[:, :], iota[:, 0:W]))
            step(dve.tensor_copy(base_i[:, :], base_row[:, 0, :]))
            step(dve.tensor_copy(base_row[:, 1, :], base_row[:, 0, :]))
            first_hots(1, 0)

            def tile_sums(t):
                for h in range(H):
                    dve.bn_stats(bn6[:, h, ds(t, 1), :].rearrange("p a s -> p (a s)"),
                                 acc[:, h, ds(t * T, T)]).then_inc(bn_step, 1)

            with dve.Fori(0, FIRST_IT) as i:
                add_hots(1, 0, i)
            with dve.Fori(0, GROUPS) as g:
                flags = load_flags(taken[0:1, ds(g, 1), 0:GT + 1].rearrange("p a q -> p (a q)"))
                for r in range(GIT):
                    for j, (first, _) in enumerate(TURNS):
                        if first // WPI == r:
                            with dve.If(flags[j + 1] > 0):
                                tile_sums(g * GT + j)
                    add_hots(1, 0, g * GIT + (FIRST_IT + r))
            with dve.Fori(SINGLE_IT, NIT) as i:
                took, take = load_two(taken_one[0:1, ds(i - SINGLE_IT, 1), 0:2].rearrange("p a q -> p (a q)"))
                with dve.If(take > 0):
                    tile_sums(i - LAG)
                add_hots(1, 0, i)
            more_passes(1, n_pass)
            with dve.Fori(t0, NT) as t:
                tile_sums(t)
            dve.wait_ge(bn_step, H * NT)
            for h in range(H):
                last = dve.bn_aggr(bn[:, h, 0:2], bn6[:, h, :, :].rearrange("p q s -> p (q s)"))
            step(last)
            dve.tensor_scalar(bn[:, :, 2], bn[:, :, 1], EPS, None, ALU.add).then_inc(bn_var, 1)
            dve.wait_ge(bn_std, 1)
            dve.wait_ge(small_in, 96)
            step(dve.reciprocal(bn[:, :, 4], bn[:, :, 3]))
            step(dve.tensor_tensor(bn[:, :, 5], bn[:, :, 4], gb[:, 0, :], ALU.mult))
            step(dve.tensor_tensor(bn[:, :, 7], bn[:, :, 0], bn[:, :, 5], ALU.mult))
            dve.tensor_tensor(bn[:, :, 6], gb[:, 1, :], bn[:, :, 7], ALU.subtract).then_inc(bn_ready, 1)
            for n, (a, b) in enumerate(PAIRS):
                dve.wait_ge(fin_turned, n + 1)
                dve.tensor_tensor(x_sb[0:T, a:b, :], x_sb[0:T, a:b, :],
                                  bank[n % 4][0:T, 0:F * (b - a)].rearrange("p (t f) -> p t f", f=F),
                                  ALU.add).then_inc(fin_ready, 1)

        @block.tensor
        def _(pe):
            pe.wait_ge(consts, 4)
            for b, a in ((2, rel_g), (3, ew_g), (4, src_g), (5, idx2_g)):
                if b < 4:
                    pe.wait_ge(pads_ready, b - 1)
                else:
                    pe.wait_ge(edges_ready, 2)
                for k in range(BPW):
                    last = pe.transpose(bank[b][:, NG * k:NG * (k + 1)], a[:, P * k:P * (k + 1)], ident[0:NG, 0:NG])
                last.then_inc(edges_turned, 1)
            pe.transpose(bank[6][0:1, 0:NG], span[0:NG, 0:1], ident[0:NG, 0:NG])
            pe.transpose(bank[6][0:1, P:P + NG], span[0:NG, 2:3], ident[0:NG, 0:NG]).then_inc(edges_turned, 1)
            def sum_blocks(p):
                sums = bank[0][0:W, 0:3 * NG]
                pe.matmul(sums, ones[0:1, 0:W], zrow[0:1, 0:3 * NG], start=True, stop=False)
                for k in range(BPW):
                    pe.wait_ge(chunk_ready, p * BPW + (k + 1))
                    pe.sem_inc(gate_pe, 1)
                    for g in range(NG):
                        last = pe.matmul(sums.rearrange("w (s g) -> w s g", g=NG)[:, :, g], oh_b[k % 2][:, :, g],
                                         ewp[:, :, k * NG + g], start=False, stop=False)
                    last.then_inc(chunk_summed, 1)
                pe.matmul(sums, ones[0:1, 0:W], zrow[0:1, 0:3 * NG], start=False, stop=True).then_inc(deg_summed, 1)

            def turn_degrees(p):
                pe.wait_ge(degw_ready, p + 1)
                pe.sem_inc(gate_pe, 1)
                pe.transpose(bank[1][0:NG, 0:W], deg_w, ident[0:W, 0:W]).then_inc(degw_turned, 1)

            def place(p):
                pe.wait_ge(spread_ready, p * 2 + 2)
                pe.sem_inc(gate_pe, 1)
                at = bank[6][0:T, 0:3 * NT]
                pe.matmul(at, ones[0:1, 0:T], zrow[0:1, 0:3 * NT], start=True, stop=False)
                for w in range(W):
                    pe.matmul(at, base_lo[:, W - 1 - w:W - 1 - w + T], spread[:, :, w, 1:HC], start=False, stop=False)
                    if w:
                        pe.matmul(at[0:w, :], base_lo[:, W - 1 - w + T:W - 1 + T], spread[:, :, w, 0:NT],
                                  start=False, stop=False)
                pe.matmul(at, ones[0:1, 0:T], zrow[0:1, 0:3 * NT], start=False, stop=True).then_inc(placed, 1)

            def turn_gru(n):
                k, g = n // 4, n % 4
                pe.wait_ge(turned_kept, n + 1)
                for q in range(4 * g, min(4 * g + 4, 14)):
                    a = gru_raw[:, q, P * k:P * (k + 1)] if q < 12 else h0[:, q - 12, P * k:P * (k + 1)]
                    last = pe.transpose(bank[2 + n % 4][:, P * (q - 4 * g):P * (q - 4 * g + 1)], a, ident[:, :])
                last.then_inc(gru_turned, 1)

            pe.sem_inc(chunk_summed, 2)
            sum_blocks(0)
            pe.wait_ge(gru_in, 48)
            for n in range(4):
                turn_gru(n)
            turn_degrees(0)
            for n in range(4, 8):
                turn_gru(n)
            pe.wait_ge(passes_ready, 1)
            place(0)
            n_pass = pe.value_load(passes[0:1, 0:1], min_val=1, max_val=NPASS)
            with pe.If(n_pass > 1):
                with pe.Fori(1, n_pass) as p:
                    sum_blocks(p)
                    turn_degrees(p)
                    place(p)
            pe.sem_inc(gate_pe, 1)
            pe.wait_ge(turned_kept, 12)
            pe.wait_ge(small_in, 96)
            for m in range(H):
                hs = [gru_t[:, k, 12 * P + P * m:12 * P + P * (m + 1)] for k in range(H)]
                for k in range(H):
                    pe.matmul(bank[4 + m][:, :], hs[k], gru_t[:, k, 3 * F:5 * F], start=(k == 0), stop=False)
                pe.matmul(bank[4 + m][:, :], ones[:, :], brow[:, 0, 0:2 * F], start=False, stop=False)
                pe.matmul(bank[4 + m][:, :], ones[:, :], brow[:, 1, 0:2 * F], start=False, stop=True)
                o = bank[7][:, F * m:F * (m + 1)]
                for k in range(H):
                    pe.matmul(o, hs[k], gru_t[:, k, 5 * F:6 * F], start=(k == 0), stop=False)
                last = pe.matmul(o, ones[:, :], brow[:, 1, 2 * F:3 * F], start=False, stop=True)
            last.then_inc(gh_ready, 1)
            for t in range(NT):
                if t == 4:
                    pe.wait_ge(score_ready, 1)
                    pe.transpose(bank[6][0:NT, 0:T], score[0:T, 1, :], ident[0:T, 0:T]).then_inc(score_turned, 1)
                if t % 5 == 4:
                    pe.wait_ge(hp_ready, t // 5 + 1)
                else:
                    pe.wait_ge(hp_ready_d, 4 * (t // 5) + t % 5 + 1)
                if t >= 4:
                    pe.wait_ge(acc_init, t - 3)
                for h in range(H):
                    last = pe.transpose(bank[t % 4][:, T * h:T * (h + 1)], hp[0:T, t, P * h:P * (h + 1)],
                                        ident[0:T, 0:T])
                last.then_inc(hp_turned, 1)
            pe.wait_ge(acc_init, NT)

            def sum_window(L, w, i, v):
                if isinstance(i, int) and 0 < i <= GRU_IT:
                    pe.wait_ge(win_added[L], (i - 1) * WPI + (v + 1))
                    pe.wait_ge(hot_ready_a, (i - 1) * WPI + (v + 1))
                else:
                    pe.wait_ge(hot_ready[L], (w * (NIT + 1) + i) * WPI + (v + 1))
                pe.wait_ge(gathered[L][v], (w * NIT + i) * (16 * BPW) + 16 * BPW)
                for h in range(H):
                    for k in range(BPW):
                        last = pe.matmul(win[v][:, h, :], ring[:, BPW * v + k, P * h:P * (h + 1)],
                                         onehot[:, v, k, :], start=(k == 0), stop=(k == BPW - 1))
                last.then_inc(win_summed[L], 1)

            def sum_windows(L, w, i):
                for v in range(WPI):
                    sum_window(L, w, i, v)

            def sum_more(L, n_pass):
                with pe.If(n_pass > 1):
                    with pe.Fori(1, n_pass) as w:
                        with pe.Fori(0, NIT) as i:
                            sum_windows(L, w, i)
                pe.sem_inc(gate_pe, 1)

            pe.wait_ge(consts, 7)

            def count_masks(t):
                pe.wait_ge(mask_ready, t + 1)
                if t >= 2:
                    pe.wait_ge(counts_added, t - 1)
                for u in range(t + 1, NT):
                    last = pe.matmul(beaten[t % 2][:, u:u + 1], mask[t % 2][0:T, T * (u - t):T * (u - t + 1)],
                                     ones_b[0:T, :], start=True, stop=True)
                last.then_inc(mask_used, 1)

            def pick_row(t):
                pe.wait_ge(rank_hot, t + 1)
                for h in range(H):
                    last = pe.matmul(bank[6 + h][:, 0:F], h_sb[0:T, t, P * h:P * (h + 1)], oh_rank[0:T, t % 4, :],
                                     start=(t == 0), stop=(t == NT - 1))
                last.then_inc(rank_used, 1)

            pe.sem_inc(prod_ready, 4)
            pe.sem_inc(tile_mul, 1)
            pe.sem_inc(h2_turned, 1)
            pe.wait_ge(score_kept, 1)
            pe.wait_ge(gh_kept, 1)
            before, hots_before = COMPARED_FIRST, []
            for i in range(GRU_IT):
                for v in range(WPI):
                    sum_window(0, 0, i, v)
                    at = i * WPI + v
                    for t in before:
                        if t < NT - 1:
                            count_masks(t)
                    for t in hots_before:
                        pick_row(t)
                    before, hots_before = COMPARED[at] if at < len(COMPARED) else [], HOT_RANKS.get(at, [])
            def gates(m):
                for k in range(H):
                    last = pe.matmul(bank[4 + m][:, :], xt[:, k, P * m:P * (m + 1)], gru_t[:, k, 0:2 * F],
                                     start=(k == 0), stop=(k == H - 1))
                last.then_inc(gates_ready, 1)

            def candidate(m):
                o = bank[6 + m][:, 0:F]
                for k in range(H):
                    pe.matmul(o, xt[:, k, P * m:P * (m + 1)], gru_t[:, k, 2 * F:3 * F], start=(k == 0), stop=False)
                pe.matmul(o, ones[:, :], brow[:, 0, 2 * F:3 * F], start=False, stop=True).then_inc(gates_ready, 1)

            sum_window(0, 0, GRU_IT, 0)
            pe.wait_ge(xt_kept, 2)
            gates(0)
            sum_window(0, 0, GRU_IT, 1)
            candidate(0)
            gates(1)
            sum_window(0, 0, GRU_IT, 2)
            candidate(1)
            sum_window(0, 0, GRU_IT, 3)

            def times_w(t):
                pe.wait_ge(w_ready, 2)
                pe.wait_ge(tile_in, t + 1)
                for h in range(H):
                    last = pe.matmul(bank[4][0:T, 0:F], s_tile[:, h, :], w_new[:, h, :],
                                     start=(h == 0), stop=(h == H - 1))
                last.then_inc(tile_mul, 1)

            def turn_h2(t):
                pe.wait_ge(h2_ready, t + 2)
                for h in range(H):
                    last = pe.transpose(bank[5][:, T * h:T * (h + 1)], h2[0:T, P * h:P * (h + 1)], ident[0:T, 0:T])
                last.then_inc(h2_turned, 1)

            def product(t, q):
                if q == 0:
                    pe.wait_ge(wrel_in, 32)
                    pe.wait_ge(h2_kept, t + 2)
                pe.wait_ge(prod_kept_a if q % 2 == 0 else prod_kept_d, t * 2 + (q // 2 + 3))
                for k in range(H):
                    last = pe.matmul(bank[6 + q % 2][0:T, :], h2_t[:, k, :], wr[:, k, 512 * q:512 * (q + 1)],
                                     start=(k == 0), stop=(k == H - 1))
                last.then_inc(prod_ready, 1)

            load_flags, load_two = loader(pe, "flag", GT + 1, 0, 1), loader(pe, "two", 2, 0, 1)
            t0 = pe.value_load(passes[0:1, 1:2], min_val=0, max_val=EARLY)
            more = pe.value_load(passes[0:1, 2:3], min_val=0, max_val=1)
            pending = pe.value_load(taken_one[0:1, EARLY - GROUPS * GT - 1, 1:2], min_val=0, max_val=1)

            def turn(i0, first, end, t, take, took):
                for n, s in enumerate(range(first, end)):
                    sum_window(0, 0, i0 + s // WPI, s % WPI)
                    if n == 1:
                        with pe.If(take > 0):
                            times_w(t)
                    if n < 3:
                        with pe.If(took > 0):
                            product(t - 1, n)
                with pe.If(took > 0):
                    product(t - 1, 3)
                with pe.If(take > 0):
                    turn_h2(t)
                pe.sem_inc(gate_pe, 1)

            with pe.Fori(0, GROUPS) as g:
                flags = load_flags(taken[0:1, ds(g, 1), 0:GT + 1].rearrange("p a q -> p (a q)"))
                for j, (first, end) in enumerate(TURNS):
                    turn(g * GIT + FIRST_IT, first, end, g * GT + j, flags[j + 1], flags[j])
            with pe.Fori(SINGLE_IT, NIT) as i:
                took, take = load_two(taken_one[0:1, ds(i - SINGLE_IT, 1), 0:2].rearrange("p a q -> p (a q)"))
                turn(i, 0, WPI, i - LAG, take, took)
            sum_more(0, n_pass)
            with pe.If(pending > 0):
                for q in range(2):
                    product(EARLY - 1, q)
            pe.sem_inc(gate_pe, 1)
            times_w(t0)
            with pe.If(pending > 0):
                for q in range(2, 4):
                    product(EARLY - 1, q)
            pe.sem_inc(gate_pe, 1)
            with pe.If(more > 0):
                with pe.Fori(t0, NT - 1) as t:
                    turn_h2(t)
                    times_w(t + 1)
                    for q in range(4):
                        product(t, q)
            pe.sem_inc(gate_pe, 1)
            turn_h2(NT - 1)
            for q in range(4):
                product(NT - 1, q)

            with pe.Fori(0, NIT) as i:
                sum_windows(1, 0, i)
            sum_more(1, n_pass)
            for n, (a, b) in enumerate(PAIRS):
                pe.wait_ge(fin_in, sum(c < b for c in CUTS))
                if n >= 4:
                    pe.wait_ge(fin_ready, n - 3)
                for t in range(a, b):
                    for h in range(H):
                        last = pe.transpose(bank[n % 4][0:T, F * (t - a) + P * h:F * (t - a) + P * (h + 1)],
                                            acc[:, h, T * t:T * (t + 1)], ident[:, :])
                last.then_inc(fin_turned, 1)


_INS = ['x', 'src', 'dst', 'edge_type_8', 'edge_weight', 'L0_gnn_initial_weight', 'L0_gnn_pool_p', 'L0_gnn_gru_W_ih',
        'L0_gnn_gru_W_hh', 'L0_gnn_gru_b_ih', 'L0_gnn_gru_b_hh', 'L1_gnn_weight', 'L1_gnn_gamma', 'L1_gnn_beta']
_OUTS = [((N, F), 'float32')]


def kernel(**inputs):
    import numpy as _np
    import concourse.bacc as _bacc
    from concourse import mybir as _mybir
    from concourse.bass_utils import run_bass_kernel_spmd as _run

    nc = _bacc.Bacc("TRN2", target_bir_lowering=False, num_devices=1)
    arrays, args = {}, []
    for name in _INS:
        a = _np.ascontiguousarray(inputs[name])
        arrays[f"in_{name}_dram"] = a
        args.append(nc.dram_tensor(f"in_{name}_dram", a.shape, _mybir.dt.from_np(a.dtype), kind="ExternalInput").ap())
    for i, (shape, dtype) in enumerate(_OUTS):
        dt = _mybir.dt.from_np(_np.dtype(dtype))
        args.append(nc.dram_tensor(f"out_{i}_dram", shape, dt, kind="ExternalOutput").ap())
    gnn_kernel(nc, *args)
    r = _run(nc, [arrays], core_ids=[0])
    return r.results[0]["out_0_dram"]
```
